# Optimizing a Trainium2 kernel written in Bass

```python
import numpy as np
import jax
import jax.numpy as jnp

def _softmax(x, axis=-1):
    return jax.nn.softmax(x, axis=axis)

def _gelu(x):
    return jax.nn.gelu(x, approximate=True)

def _silu(x):
    return jax.nn.silu(x)

def _sigmoid(x):
    return jax.nn.sigmoid(x)

def _layernorm(x, axis=-1, eps=1e-05):
    m = jnp.mean(x, axis=axis, keepdims=True)
    v = jnp.var(x, axis=axis, keepdims=True)
    return (x - m) / jnp.sqrt(v + eps)

def _scatter_add(tgt, idx, src, axis=0):
    return tgt.at[idx].add(src)

def _segment_sum(src, seg, n):
    return jax.ops.segment_sum(src, seg, n)
kernel_name = 'mk_xattn_ffn_d1_seqx_r8_439aa6'

def setup_inputs(seed: int=0):
    np.random.seed(seed)
    _w = jnp.asarray

    def _rec_inputs():
        import jax
        import jax.numpy as jnp
        _rk = jax.random.key(seed)
        x = -0.000929 + 1 * jax.random.normal(jax.random.fold_in(_rk, 1), (8, 256, 128), jnp.float32)
        _lenS = 256 - jax.random.randint(jax.random.fold_in(_rk, 7), (8,), 0, max(1, 256 // 4) + 1, jnp.int32)
        _lenS2 = 512 - jax.random.randint(jax.random.fold_in(_rk, 8), (8,), 0, max(1, 512 // 4) + 1, jnp.int32)
        _ctx_1024P = jax.random.normal(jax.random.fold_in(_rk, 11), (8, 16, 128), jnp.float32)
        _ctx_1024c = jax.random.dirichlet(jax.random.fold_in(_rk, 511), 0.3 * jnp.ones((16,), jnp.float32), (8, 512))
        _ctx_1024t = jnp.einsum('bsk,bkd->bsd', _ctx_1024c, _ctx_1024P)
        _ctx_1024t = _ctx_1024t * jax.lax.rsqrt(jnp.mean(jnp.square(_ctx_1024t)) + 1e-12) * 0.953939
        ctx_1024 = -1.52775e-05 + 0.999936 * (_ctx_1024t + 0.3 * jax.random.normal(jax.random.fold_in(_rk, 611), (8, 512, 128), jnp.float32))
        return (x, ctx_1024)
    x, ctx_1024 = _rec_inputs()

    def _L0_xattn_setup():
        import jax, jax.numpy as jnp
        import numpy as np
        B, N, L, D, H = (8, 128, 512, 128, 16)
        key = jax.random.key(seed)
        ks = jax.random.split(key, 7)
        s = 1.0 / np.sqrt(D)
        return {'q': jax.random.normal(ks[0], (B, N, D), dtype=jnp.float32), 'k': jax.random.normal(ks[1], (B, L, D), dtype=jnp.float32), 'v': jax.random.normal(ks[2], (B, L, D), dtype=jnp.float32), 'Wq': jax.random.normal(ks[3], (D, D), dtype=jnp.float32) * s, 'Wk': jax.random.normal(ks[4], (D, D), dtype=jnp.float32) * s, 'Wv': jax.random.normal(ks[5], (D, D), dtype=jnp.float32) * s, 'Wo': jax.random.normal(ks[6], (D, D), dtype=jnp.float32) * s}
    _L0_xattn_all = _L0_xattn_setup()
    _L0_xattn_in = {k: v for k, v in _L0_xattn_all.items() if k in ('Wq', 'Wk', 'Wv', 'Wo')}
    del _L0_xattn_all

    def _L0_ffn_setup():
        import jax, jax.numpy as jnp
        import numpy as np
        B, T, D, E, H = (8, 256, 128, 8, 32)
        LN_EPS = 1e-05
        key = jax.random.key(seed)
        ks = jax.random.split(key, 4)
        return {'x': jax.random.normal(ks[0], (B, T, D), dtype=jnp.float32), 'Wg': jax.random.normal(ks[1], (E, D), dtype=jnp.float32) * 0.02, 'ln_scale': jnp.ones((E, D), dtype=jnp.float32), 'ln_bias': jnp.zeros((E, D), dtype=jnp.float32), 'W1': jax.random.normal(ks[2], (E, D, H), dtype=jnp.float32) * 0.02, 'b1': jnp.zeros((E, H), dtype=jnp.float32), 'W2': jax.random.normal(ks[3], (E, H, D), dtype=jnp.float32) * 0.02, 'b2': jnp.zeros((E, D), dtype=jnp.float32)}
    _L0_ffn_all = _L0_ffn_setup()
    _L0_ffn_in = {k: v for k, v in _L0_ffn_all.items() if k in ('Wg', 'ln_scale', 'ln_bias', 'W1', 'b1', 'W2', 'b2')}
    del _L0_ffn_all
    return {'x': x, 'ctx_1024': ctx_1024, 'L0_xattn_Wq': _L0_xattn_in['Wq'], 'L0_xattn_Wk': _L0_xattn_in['Wk'], 'L0_xattn_Wv': _L0_xattn_in['Wv'], 'L0_xattn_Wo': _L0_xattn_in['Wo'], 'L0_ffn_Wg': _L0_ffn_in['Wg'], 'L0_ffn_ln_scale': _L0_ffn_in['ln_scale'], 'L0_ffn_ln_bias': _L0_ffn_in['ln_bias'], 'L0_ffn_W1': _L0_ffn_in['W1'], 'L0_ffn_b1': _L0_ffn_in['b1'], 'L0_ffn_W2': _L0_ffn_in['W2'], 'L0_ffn_b2': _L0_ffn_in['b2']}

def reference(x, ctx_1024, L0_xattn_Wq, L0_xattn_Wk, L0_xattn_Wv, L0_xattn_Wo, L0_ffn_Wg, L0_ffn_ln_scale, L0_ffn_ln_bias, L0_ffn_W1, L0_ffn_b1, L0_ffn_W2, L0_ffn_b2):
    import jax
    import jax.numpy as jnp

    def _L0_xattn_ref(q, k, v, Wq, Wk, Wv, Wo):
        import jax, jax.numpy as jnp
        import numpy as np
        B, N, L, D, H = (8, 128, 512, 128, 16)
        Bq, Nq, Dm = q.shape
        Lk = k.shape[1]
        Hh = H
        Dh = Dm // Hh
        scale = Dm ** (-0.5)
        qh = (q @ Wq.T).reshape(Bq, Nq, Hh, Dh).transpose(0, 2, 1, 3)
        kh = (k @ Wk.T).reshape(Bq, Lk, Hh, Dh).transpose(0, 2, 1, 3)
        vh = (v @ Wv.T).reshape(Bq, Lk, Hh, Dh).transpose(0, 2, 1, 3)
        attn = jnp.einsum('bhnc,bhlc->bhnl', qh * scale, kh)
        attn = jax.nn.softmax(attn, axis=2)
        attn = attn / jnp.sum(attn, axis=-1, keepdims=True)
        out = jnp.einsum('bhnl,bhlc->bhnc', attn, vh)
        out = out.transpose(0, 2, 1, 3).reshape(Bq, Nq, Dm)
        return out @ Wo.T

    def _L0_ffn_ref(x, Wg, ln_scale, ln_bias, W1, b1, W2, b2):
        import jax, jax.numpy as jnp
        import numpy as np
        B, T, D, E, H = (8, 256, 128, 8, 32)
        LN_EPS = 1e-05
        Bs, Ts, Ds = x.shape
        xt = x.reshape(Bs * Ts, Ds)
        logits = xt @ Wg.T
        top1 = jnp.argmax(logits, axis=-1)
        mu = jnp.mean(xt, axis=-1, keepdims=True)
        var = jnp.mean(jnp.square(xt - mu), axis=-1, keepdims=True)
        xhat = (xt - mu) * jax.lax.rsqrt(var + LN_EPS)
        n_experts = Wg.shape[0]

        def body(y, p):
            s_e, b_e, w1, bb1, w2, bb2, eid = p
            h = jax.nn.gelu((xhat * s_e + b_e) @ w1 + bb1, approximate=False)
            out = h @ w2 + bb2
            mask = (top1 == eid)[:, None].astype(out.dtype)
            return (y + mask * out, None)
        y0 = jnp.zeros_like(xt)
        y, _ = jax.lax.scan(body, y0, (ln_scale, ln_bias, W1, b1, W2, b2, jnp.arange(n_experts)))
        return y.reshape(Bs, Ts, Ds)
    x = x + _L0_xattn_ref(_layernorm(x, axis=-1), ctx_1024, ctx_1024, L0_xattn_Wq, L0_xattn_Wk, L0_xattn_Wv, L0_xattn_Wo)
    x = x + _L0_ffn_ref(_layernorm(x, axis=-1), L0_ffn_Wg, L0_ffn_ln_scale, L0_ffn_ln_bias, L0_ffn_W1, L0_ffn_b1, L0_ffn_W2, L0_ffn_b2)
    return x

_drawn_inputs = setup_inputs


def setup_inputs(seed=0):
    import zlib

    import numpy as np

    out = dict(_drawn_inputs(seed))
    spreads = {'L0_ffn_ln_scale': (1.0, 0.6),
     'L0_ffn_ln_bias': (0.0, 0.8),
     'L0_ffn_b1': (0.0, 0.8),
     'L0_ffn_b2': (0.0, 0.1)}
    factors = {'L0_ffn_W1': 4.464, 'L0_ffn_W2': 4.061}
    for name, (base, spread) in spreads.items():
        noise = np.random.default_rng([zlib.crc32(name.encode()), seed]).standard_normal(out[name].shape)
        drawn = base * np.exp(spread * noise) if base else spread * noise
        out[name] = jnp.asarray(drawn.astype(out[name].dtype))
    for name, factor in factors.items():
        out[name] = (out[name] * factor).astype(out[name].dtype)
    return out
```

```python
import concourse.bass as bass
from concourse import mybir
from contextlib import ExitStack

F32 = mybir.dt.float32
BF16 = mybir.dt.bfloat16
ALU = mybir.AluOpType
ACT = mybir.ActivationFunctionType
AX = mybir.AxisListType

P = 128
HEADS = 16
LN_EPS = 1e-5
PARTS = 3
GH = 4
DVE_BANKS = 4


def cross_attention_moe(nc, x, ctx, Wq, Wk, Wv, Wo, Wg, ln_scale, ln_bias, W1, b1, W2, b2, out):
    B, N, D = x.shape
    L = ctx.shape[1]
    C = D // HEADS
    NB, LB = N // P, L // P
    GROUPS = HEADS // GH
    BANKS = GH * LB // 2
    KROWS = PARTS * PARTS * C
    TERM = PARTS * C
    E, H = b1.shape
    EH = E * H
    HB = EH // P
    T = B * NB
    SCALE = float(D) ** -0.5
    RING = DVE_BANKS
    LASTG = B * GROUPS
    HALF = HEADS // 2

    k_parts_dram = nc.dram_tensor("k_parts_dram", [PARTS, P, L], BF16, kind="Internal").ap()
    q_parts_dram = nc.dram_tensor("q_parts_dram", [PARTS, P, N], BF16, kind="Internal").ap()

    with ExitStack() as stack:
        def sb(name, shape, dt=F32):
            return stack.enter_context(nc.sbuf_tensor(name, shape, dt))

        def bank(name):
            return stack.enter_context(nc.psum_tensor(name, [P, 512], F32))

        def sem(name):
            return stack.enter_context(nc.semaphore(name))

        ident = sb("ident", [P, P])
        ident_bf = sb("ident_bf", [P, P], BF16)
        w_in = sb("w_in", [P, 4, D])
        w_t = sb("w_t", [P, 4, D])
        x_all = sb("x_all", [P, B, NB, D])
        x2_all = sb("x2_all", [P, B, NB, D])
        ctx_in = sb("ctx_in", [P, LB, D])
        ctx_t = sb("ctx_t", [P, L])
        stats = sb("stats", [P, NB, 6])
        mean_var = sb("mean_var", [P, NB, 2])
        rstd = sb("rstd", [P, NB])
        minus_half = sb("minus_half", [P, T])
        eps = sb("eps", [P, NB])
        zero = sb("zero", [P, 1])
        xn = sb("xn", [P, NB, D])
        xn_t = sb("xn_t", [P, N])
        kf = sb("kf", [P, L])
        qf = sb("qf", [P, N])
        k_rest = sb("k_rest", [P, L])
        q_rest = sb("q_rest", [P, N])
        k_parts = sb("k_parts", [P, PARTS, L], BF16)
        q_parts = sb("q_parts", [P, PARTS, N], BF16)
        k_stack = sb("k_stack", [P, HEADS, L], BF16)
        q_stack = sb("q_stack", [P, HEADS, N], BF16)
        v_ones = sb("v_ones", [P, LB, HEADS, C + 1])
        v_hat = sb("v_hat", [P, 2, GH, LB, 32])
        neg_max = sb("neg_max", [P, BANKS, 2])
        row_sum = sb("row_sum", [P, 2, GH * LB])
        recip_sum = sb("recip_sum", [P, 2, GH * LB])
        expd = sb("expd", [P, 2, GH, LB, N])
        o_sb = sb("o_sb", [P, N])
        recip_den = sb("recip_den", [P, NB, GH])
        o_n = sb("o_n", [P, NB, D])
        o_t = sb("o_t", [P, N])

        wg_t = sb("wg_t", [P, E])
        scale_t = sb("scale_t", [P, E])
        bias_t = sb("bias_t", [P, E])
        w1_raw = sb("w1_raw", [P, E, H])
        w1_s = sb("w1_s", [P, E, H])
        b1_col = sb("b1_col", [P, HB])
        w2_sb = sb("w2_sb", [P, HB, D])
        b2_sb = sb("b2_sb", [E, D])
        own = sb("own", [P, HB, E])
        ones_e = sb("ones_e", [P, HB, E])
        own_bias = sb("own_bias", [P, HB, E])
        bias_sum = sb("bias_sum", [P, HB])
        hid_bias = sb("hid_bias", [P, HB])
        fstats = sb("fstats", [P, T, 6])
        fmv = sb("fmv", [P, T, 2])
        frow = sb("frow", [P, 6, T])
        xh = sb("xh", [P, 4, D])
        xh_t = sb("xh_t", [P, 2, 512])
        logits = sb("logits", [P, 4, E])
        top = sb("top", [P, 4])
        first = sb("first", [P, 4, E])
        ftop = sb("ftop", [P, 4])
        order = sb("order", [P, E])
        onehot = sb("onehot", [P, 4, E], BF16)
        hid = sb("hid", [P, 2, HB, 512])
        hid_m = sb("hid_m", [P, 2, HB, 512])
        mask_t = sb("mask_t", [E, 2, 512])
        mask_bf = sb("mask_bf", [E, 2, 512], BF16)
        expand = sb("expand", [E, HB, P], BF16)
        y_sb = sb("y_sb", [P, 2, 4, D])

        S = [bank(f"scores{i}") for i in range(RING)]
        O = bank("o_acc")
        TB = bank("transposes")
        PB = bank("projections")
        M = bank("mixed")

        (consts_ready, ident0, w_loaded, x0_loaded, x_rest_loaded, ctx_loaded, small_loaded, w_transposed,
         w_ready, stats_done, moments_ready, eps_added, rstd_ready, xn_ready, xn_transposed, xn_t_ready,
         ctx_transposed, ctx_t_ready, k_projected, k_copied, q_projected, q_copied, v_projected, v_copied,
         k_split, q_split, k_parts_ready, q_parts_ready, k_stored, q_stored, half0_loaded, half1_loaded,
         scores_ready, max_ready, exps_done, recip_ready, v_hat_ready, pv_done, o_copied, o_transposed,
         den_ready, o_normed, o_t_transposed, o_t_copied, wo_projected, x2_ready) = [
            sem(n) for n in (
                "consts_ready ident0 w_loaded x0_loaded x_rest_loaded ctx_loaded small_loaded w_transposed "
                "w_ready stats_done moments_ready eps_added rstd_ready xn_ready xn_transposed xn_t_ready "
                "ctx_transposed ctx_t_ready k_projected k_copied q_projected q_copied v_projected v_copied "
                "k_split q_split k_parts_ready q_parts_ready k_stored q_stored half0_loaded half1_loaded "
                "scores_ready max_ready exps_done recip_ready v_hat_ready pv_done o_copied o_transposed "
                "den_ready o_normed o_t_transposed o_t_copied wo_projected x2_ready").split()]
        (f_stats, f_moments, f_small, xh_ready, xh_transposed, xh_t_ready, hid_projected, gelu_done,
         logits_projected, logits_copied, top_done, first_done, ftop_done, onehot_ready, masks_projected, mask_t_ready,
         hid_masked, y_projected, y_ready, y_stored0, y_stored1, w1_scaled, bias_projected, bias_masked, bias_summed,
         hid_bias_ready) = [
            sem(n) for n in (
                "f_stats f_moments f_small xh_ready xh_transposed xh_t_ready hid_projected gelu_done "
                "logits_projected logits_copied top_done first_done ftop_done onehot_ready masks_projected mask_t_ready "
                "hid_masked y_projected y_ready y_stored0 y_stored1 w1_scaled bias_projected bias_masked bias_summed "
                "hid_bias_ready").split()]

        y_stored = (y_stored0, y_stored1)

        def need(eng, semaphore, value):
            if not isinstance(value, int) or value > 0:
                eng.wait_ge(semaphore, value)

        LOOPS = B - 2

        def schedule(eng, step):
            step(0, 0, 0)
            step(1, 0, 1)
            with eng.Fori(0, LOOPS) as r:
                step(r * GROUPS + 2, r, 2)
                step(r * GROUPS + 3, r, 3)
                step(r * GROUPS + 4, r + 1, 0)
                step(r * GROUPS + 5, r + 1, 1)
            for G in range(LOOPS * GROUPS + 2, LASTG + 2):
                step(G, G // GROUPS, G % GROUPS)

        def stages_next(G):
            return not isinstance(G, int) or G // GROUPS + 1 < B

        def live(G):
            return not isinstance(G, int) or 0 <= G < LASTG

        block = stack.enter_context(nc.Block())

        @block.sync
        def _(sp):
            def load_ctx(b):
                sp.dma_start(ctx_in[:, :, :], ctx[b].rearrange("(k p) d -> p k d", p=P)).then_inc(ctx_loaded, 16)

            def load_half(half, loaded):
                heads = slice(half * HALF, (half + 1) * HALF)
                kd = k_parts_dram.rearrange("b (c h) l -> (b c) h l", h=HEADS)[:, heads, :]
                for a in range(PARTS):
                    sp.dma_start(k_stack[a * TERM:(a + 1) * TERM, heads, :], kd).then_inc(loaded, 16)
                for a in range(PARTS):
                    qd = q_parts_dram[a].rearrange("(c h) n -> c h n", h=HEADS)[:, heads, :]
                    for t in range(PARTS):
                        row = a * TERM + t * C
                        sp.dma_start(q_stack[row:row + C, heads, :], qd).then_inc(loaded, 16)

            def store_parts(b):
                need(sp, half1_loaded, b * 16 * 12)
                sp.wait_ge(k_parts_ready, b + 1)
                sp.dma_start(k_parts_dram.rearrange("a p l -> p a l"), k_parts[:, :, :]).then_inc(k_stored, 16)
                sp.wait_ge(q_parts_ready, b + 1)
                sp.dma_start(q_parts_dram.rearrange("a p n -> p a n"), q_parts[:, :, :]).then_inc(q_stored, 16)
                sp.wait_ge(k_stored, (b + 1) * 16)
                sp.wait_ge(q_stored, (b + 1) * 16)

            sp.dma_start(x_all[:, 0, :, :], x[0].rearrange("(s p) d -> p s d", p=P)).then_inc(x0_loaded, 16)
            load_ctx(0)
            for i, w in enumerate((Wq, Wk, Wv, Wo)):
                sp.dma_start(w_in[:, i, :], w).then_inc(w_loaded, 16)
            for b in range(1, B):
                sp.dma_start(x_all[:, b, :, :], x[b].rearrange("(s p) d -> p s d", p=P)).then_inc(x_rest_loaded, 16)
            sp.wait_ge(ctx_transposed, 1)
            load_ctx(1)
            store_parts(0)
            load_half(0, half0_loaded)
            load_half(1, half1_loaded)
            with nc.allow_non_contiguous_dma(reason="small weights"):
                sp.dma_start(wg_t[:, :], Wg.rearrange("e d -> d e")).then_inc(small_loaded, 16)
                sp.dma_start(scale_t[:, :], ln_scale.rearrange("e d -> d e")).then_inc(small_loaded, 16)
                sp.dma_start(bias_t[:, :], ln_bias.rearrange("e d -> d e")).then_inc(small_loaded, 16)
                sp.dma_start(w1_raw[:, :, :], W1.rearrange("e d h -> d e h")).then_inc(small_loaded, 16)
                sp.dma_start(b1_col[:, :], b1.rearrange("(a e) h -> (e h) a", a=HB)).then_inc(small_loaded, 16)
            sp.dma_start(w2_sb[:, :, :], W2.rearrange("(a e) h d -> (e h) a d", a=HB)).then_inc(small_loaded, 16)
            sp.dma_start(b2_sb[:, :], b2).then_inc(small_loaded, 16)

            def batch(b, more):
                if more:
                    sp.wait_ge(ctx_transposed, b + 2)
                    load_ctx(b + 2)
                store_parts(b + 1)
                sp.wait_ge(scores_ready, (b * GROUPS + 2) * BANKS)
                load_half(0, half0_loaded)
                sp.wait_ge(scores_ready, (b * GROUPS + 4) * BANKS)
                load_half(1, half1_loaded)

            with sp.Fori(0, B - 2) as b:
                batch(b, True)
            batch(B - 2, False)
            for c in range(T // 4):
                sp.wait_ge(y_ready, c + 1)
                sp.dma_start(out[2 * c:2 * c + 2].rearrange("b (s p) d -> p (b s) d", p=P),
                             y_sb[:, c % 2, :, :]).then_inc(y_stored[c % 2], 16)
            for stored in y_stored:
                sp.wait_ge(stored, 16 * (T // 8))

        @block.gpsimd
        def _(pool):
            for m in (ident, ident_bf):
                pool.memset(m[:, :], 0.0).then_inc(ident0, 1)
            pool.memset(own[:, :, :], 1.0).then_inc(ident0, 1)
            pool.memset(expand[:, :, :], 1.0).then_inc(ident0, 1)
            pool.memset(minus_half[:, :], -0.5).then_inc(consts_ready, 1)
            pool.memset(eps[:, :], LN_EPS).then_inc(consts_ready, 1)
            pool.memset(zero[:, :], 0.0).then_inc(consts_ready, 1)
            pool.memset(v_hat[:, :, :, :, :], 0.0).then_inc(consts_ready, 1)
            pool.memset(v_ones[:, :, :, :], 1.0).then_inc(consts_ready, 1)
            for e in range(E):
                pool.memset(order[:, e:e + 1], float(E - e)).then_inc(consts_ready, 1)
            pool.wait_ge(ident0, 4)
            for m in (ident, ident_bf):
                pool.affine_select(out=m[:, :], in_=m[:, :], compare_op=ALU.not_equal, fill=1.0, base=0,
                                   pattern=[[-1, P]], channel_multiplier=1).then_inc(consts_ready, 1)
            pool.affine_select(out=own[:, :, :], in_=own[:, :, :], compare_op=ALU.is_ge, fill=0.0, base=0,
                               pattern=[[P, HB], [-H, E]], channel_multiplier=1).then_inc(ident0, 1)
            pool.affine_select(out=expand[:, :, :], in_=expand[:, :, :], compare_op=ALU.is_ge, fill=0.0, base=0,
                               pattern=[[P, HB], [1, P]], channel_multiplier=-H).then_inc(ident0, 1)
            pool.wait_ge(ident0, 6)
            pool.affine_select(out=expand[:, :, :], in_=expand[:, :, :], compare_op=ALU.is_ge, fill=0.0, base=H - 1,
                               pattern=[[-P, HB], [-1, P]], channel_multiplier=H).then_inc(consts_ready, 1)
            pool.affine_select(out=own[:, :, :], in_=own[:, :, :], compare_op=ALU.is_ge, fill=0.0, base=H - 1,
                               pattern=[[-P, HB], [H, E]], channel_multiplier=-1).then_inc(consts_ready, 1)

            def make_rstd(b):
                pool.wait_ge(moments_ready, 2 * (b + 1))
                need(pool, xn_ready, b)
                pool.tensor_tensor(rstd[:, :], mean_var[:, :, 1], eps[:, :], ALU.add).then_inc(eps_added, 1)
                pool.wait_ge(eps_added, b + 1)
                pool.tensor_tensor(rstd[:, :], rstd[:, :], minus_half[:, 0:NB], ALU.pow).then_inc(rstd_ready, 1)

            def split(full, rest, parts, split_sem, ready, stored, b):
                need(pool, stored, 16 * b)
                zeros = zero[:, :].to_broadcast([P, full.shape[1]])
                pool.tensor_tensor(parts[:, 0, :], full[:, :], zeros, ALU.add).then_inc(split_sem, 1)
                pool.wait_ge(split_sem, 3 * b + 1)
                pool.tensor_tensor(rest[:, :], full[:, :], parts[:, 0, :], ALU.subtract).then_inc(split_sem, 1)
                pool.wait_ge(split_sem, 3 * b + 2)
                pool.tensor_tensor(parts[:, 1, :], rest[:, :], zeros, ALU.add).then_inc(split_sem, 1)
                pool.wait_ge(split_sem, 3 * b + 3)
                pool.tensor_tensor(parts[:, 2, :], rest[:, :], parts[:, 1, :], ALU.subtract).then_inc(ready, 1)

            def split_k(b):
                pool.wait_ge(k_copied, b + 1)
                split(kf, k_rest, k_parts, k_split, k_parts_ready, k_stored, b)

            def split_q(b):
                pool.wait_ge(q_copied, b + 1)
                split(qf, q_rest, q_parts, q_split, q_parts_ready, q_stored, b)

            def make_v_hat(G, b, g):
                pool.wait_ge(recip_ready, G + 1)
                pool.wait_ge(v_copied, b + 1)
                need(pool, pv_done, G - 1)
                slot = g % 2
                pool.tensor_tensor(
                    v_hat[:, slot, :, :, 0:C + 1],
                    v_ones[:, :, GH * g:GH * g + GH, :].rearrange("p l h c -> p h l c"),
                    recip_sum[:, slot, :].rearrange("p (h l) -> p h l", h=GH).unsqueeze(3)
                    .to_broadcast([P, GH, LB, C + 1]),
                    ALU.mult).then_inc(v_hat_ready, 1)

            pool.wait_ge(consts_ready, 9 + E)
            make_rstd(0)
            split_k(0)
            split_q(0)

            def step(G, b, g):
                if live(G - 1):
                    make_v_hat(G - 1, b - 1 if g == 0 else b, (g - 1) % GROUPS)
                if stages_next(G):
                    if g == 0:
                        make_rstd(b + 1)
                    if g == 1:
                        split_k(b + 1)
                    if g == 2:
                        split_q(b + 1)

            schedule(pool, step)
            mean, var = fmv[:, :, 0], fmv[:, :, 1]
            pool.wait_ge(f_moments, T)
            done = 0

            def chained(ins):
                nonlocal done
                done += 1
                ins.then_inc(f_small, 1)
                pool.wait_ge(f_small, done)

            chained(pool.tensor_scalar(frow[:, 0, :], var, LN_EPS, None, ALU.add))
            chained(pool.tensor_tensor(frow[:, 1, :], frow[:, 0, :], minus_half[:, :], ALU.pow))
            chained(pool.tensor_tensor(frow[:, 2, :], frow[:, 1, :], frow[:, 1, :], ALU.mult))
            chained(pool.tensor_tensor(frow[:, 3, :], frow[:, 2, :], var, ALU.mult))
            chained(pool.tensor_scalar(frow[:, 4, :], frow[:, 3, :], LN_EPS, None, ALU.add))
            chained(pool.tensor_tensor(frow[:, 5, :], frow[:, 4, :], minus_half[:, :], ALU.pow))
            chained(pool.tensor_tensor(frow[:, 0, :], frow[:, 5, :], frow[:, 1, :], ALU.mult))

        @block.vector
        def _(dve):
            for i in range(4):
                dve.wait_ge(w_transposed, 4)
                src = M[:, i * D:(i + 1) * D]
                dst = w_t[:, i, :]
                if i < 2:
                    src = src.rearrange("p (h c) -> p h c", h=HEADS)
                    dst = dst.rearrange("p (c h) -> p h c", h=HEADS)
                dve.tensor_copy(dst, src).then_inc(w_ready, 1)

            def x_stats(b):
                if isinstance(b, int) and b == 0:
                    dve.wait_ge(x0_loaded, 16)
                else:
                    dve.wait_ge(x_rest_loaded, 16 * (B - 1))
                    dve.wait_ge(rstd_ready, b)
                for s in range(NB):
                    dve.bn_stats(stats[:, s, :], x_all[:, b, s, :]).then_inc(stats_done, 1)

            def x_moments():
                for s in range(NB):
                    dve.bn_aggr(mean_var[:, s, :], stats[:, s, :]).then_inc(moments_ready, 1)

            def x_norm(b):
                dve.wait_ge(moments_ready, 2 * (b + 1))
                dve.wait_ge(rstd_ready, b + 1)
                need(dve, xn_transposed, b)
                for s in range(NB):
                    ins = dve.tensor_scalar(xn[:, s, :], x_all[:, b, s, :], mean_var[:, s, 0:1], rstd[:, s:s + 1],
                                            ALU.subtract, ALU.mult)
                ins.then_inc(xn_ready, 1)

            def copy_ctx_t(b):
                dve.wait_ge(ctx_transposed, b + 1)
                need(dve, v_projected, b)
                dve.tensor_copy(ctx_t[:, :], TB[:, :]).then_inc(ctx_t_ready, 1)

            def copy_k(b):
                dve.wait_ge(k_projected, b + 1)
                need(dve, k_parts_ready, b)
                dve.tensor_copy(kf[:, :], PB[:, :]).then_inc(k_copied, 1)

            def copy_xn_t(b):
                dve.wait_ge(xn_transposed, b + 1)
                need(dve, q_projected, b)
                dve.tensor_copy(xn_t[:, :], TB[:, 0:N]).then_inc(xn_t_ready, 1)

            def copy_q(b):
                dve.wait_ge(q_projected, b + 1)
                need(dve, q_parts_ready, b)
                dve.tensor_scalar(qf[:, :], PB[:, 0:N], SCALE, None, ALU.mult).then_inc(q_copied, 1)

            def copy_v(b):
                dve.wait_ge(v_projected, b + 1)
                need(dve, v_hat_ready, b * GROUPS)
                dve.tensor_copy(v_ones[:, :, :, 0:C],
                                PB[:, :].rearrange("p (l h c) -> p l h c", l=LB, h=HEADS)).then_inc(v_copied, 1)

            x_stats(0)
            dve.wait_ge(stats_done, NB)
            x_moments()
            x_norm(0)
            copy_ctx_t(0)
            copy_k(0)
            copy_xn_t(0)
            copy_q(0)

            def step(G, b, g):
                for k in range(BANKS):
                    if live(G):
                        if g == 0 and k == 2 and stages_next(G):
                            dve.wait_ge(stats_done, (b + 2) * NB)
                        dve.wait_ge(scores_ready, G * BANKS + k + 1)
                        dve.tensor_reduce(neg_max[:, k, :], S[k % RING][:, :].rearrange("p (j n) -> p j n", j=2),
                                          AX.X, ALU.max, negate=True).then_inc(max_ready, 1)
                    if k == 0 and live(G - 2):
                        dve.wait_ge(pv_done, G - 1)
                        need(dve, o_transposed, G - 2)
                        dve.tensor_copy(o_sb[:, :], O[:, 0:N]).then_inc(o_copied, 1)
                    if k == 2 and live(G - 2):
                        g2 = (g - 2) % GROUPS
                        dve.wait_ge(o_transposed, G - 1)
                        o_view = M[:, 0:NB * P].rearrange("p (s h c) -> p s h c", s=NB, h=GH)
                        dve.reciprocal(recip_den[:, :, :], o_view[:, :, :, C]).then_inc(den_ready, 1)
                        dve.wait_ge(den_ready, G - 1)
                        if g2 == 0:
                            need(dve, o_t_transposed, b)
                        dve.tensor_tensor(
                            o_n[:, :, g2 * GH * C:(g2 + 1) * GH * C].rearrange("p s (h c) -> p s h c", h=GH),
                            o_view[:, :, :, 0:C],
                            recip_den[:, :, :].unsqueeze(3).to_broadcast([P, NB, GH, C]),
                            ALU.mult).then_inc(o_normed, 1)
                    if k == 3 and live(G - 1):
                        dve.wait_ge(exps_done, G * BANKS)
                        need(dve, v_hat_ready, G - 2)
                        dve.reciprocal(recip_sum[:, (g - 1) % 2, :], row_sum[:, (g - 1) % 2, :]).then_inc(recip_ready, 1)
                    if g == 0 and live(G):
                        if k == 1 and stages_next(G):
                            x_stats(b + 1)
                        if k == 2 and stages_next(G):
                            x_moments()
                        if k == 4:
                            copy_v(b)
                        if stages_next(G):
                            if k == 5:
                                copy_ctx_t(b + 1)
                            if k == 6:
                                x_norm(b + 1)
                            if k == 7:
                                copy_k(b + 1)
                    if g == 1:
                        if stages_next(G):
                            if k == 1:
                                copy_xn_t(b + 1)
                            if k == 5:
                                copy_q(b + 1)
                        if live(G - 2) and (not isinstance(G, int) or G >= GROUPS):
                            if k == 4:
                                dve.wait_ge(o_t_transposed, b)
                                dve.tensor_copy(o_t[:, :], M[:, 0:N]).then_inc(o_t_copied, 1)
                            if k == 6:
                                dve.wait_ge(wo_projected, b)
                                dve.tensor_tensor(x2_all[:, b - 1, :, :], x_all[:, b - 1, :, :],
                                                  M[:, 0:N].rearrange("p (s d) -> p s d", s=NB),
                                                  ALU.add).then_inc(x2_ready, 1)

            schedule(dve, step)

            dve.wait_ge(small_loaded, 7 * 16)
            dve.tensor_tensor(w1_s[:, :, :], w1_raw[:, :, :], scale_t[:, :].unsqueeze(2).to_broadcast([P, E, H]),
                              ALU.mult).then_inc(w1_scaled, 1)
            dve.wait_ge(bias_projected, 1)
            dve.tensor_tensor(own_bias[:, :, :], own[:, :, :],
                              TB[:, 0:HB * E].rearrange("p (a e) -> p a e", a=HB), ALU.mult).then_inc(bias_masked, 1)
            dve.wait_ge(bias_masked, 1)
            dve.tensor_reduce(bias_sum[:, :], own_bias[:, :, :], AX.X, ALU.add).then_inc(bias_summed, 1)
            dve.wait_ge(bias_summed, 1)
            dve.tensor_tensor(hid_bias[:, :], bias_sum[:, :], b1_col[:, :], ALU.add).then_inc(hid_bias_ready, 1)
            x2_tiles = x2_all[:, :, :, :].rearrange("p b s d -> p (b s) d")
            dve.wait_ge(x2_ready, B)
            for t in range(T):
                dve.bn_stats(fstats[:, t, :], x2_tiles[:, t, :]).then_inc(f_stats, 1)
            for t in range(T):
                dve.wait_ge(f_stats, t + 1)
                dve.bn_aggr(fmv[:, t, :], fstats[:, t, :]).then_inc(f_moments, 1)
            dve.wait_ge(f_moments, T)
            dve.wait_ge(f_small, 7)

            def norm_tiles(c):
                need(dve, xh_transposed, c)
                for s in range(4):
                    t = 4 * c + s
                    ins = dve.tensor_scalar(xh[:, s, :], x2_tiles[:, t, :], fmv[:, t, 0:1], frow[:, 0, t:t + 1],
                                            ALU.subtract, ALU.mult)
                ins.then_inc(xh_ready, 1)
                dve.wait_ge(xh_transposed, c + 1)
                dve.tensor_copy(xh_t[:, c % 2, :], TB[:, :]).then_inc(xh_t_ready, 1)

            def route(c):
                dve.wait_ge(logits_projected, c + 1)
                dve.tensor_copy(logits[:, :, :], M[:, 0:4 * E].rearrange("p (s e) -> p s e", s=4)).then_inc(logits_copied, 1)
                dve.wait_ge(logits_copied, c + 1)
                dve.tensor_reduce(top[:, :], logits[:, :, :], AX.X, ALU.max).then_inc(top_done, 1)
                dve.wait_ge(top_done, c + 1)
                dve.tensor_tensor(first[:, :, :], logits[:, :, :], top[:, :].unsqueeze(2).to_broadcast([P, 4, E]),
                                  ALU.is_equal).then_inc(first_done, 1)
                dve.wait_ge(first_done, 2 * c + 1)
                dve.tensor_tensor(first[:, :, :], first[:, :, :], order[:, :].unsqueeze(1).to_broadcast([P, 4, E]),
                                  ALU.mult).then_inc(first_done, 1)
                dve.wait_ge(first_done, 2 * c + 2)
                dve.tensor_reduce(ftop[:, :], first[:, :, :], AX.X, ALU.max).then_inc(ftop_done, 1)
                dve.wait_ge(ftop_done, c + 1)
                need(dve, masks_projected, 3 * c - 2)
                dve.tensor_tensor(onehot[:, :, :], first[:, :, :], ftop[:, :].unsqueeze(2).to_broadcast([P, 4, E]),
                                  ALU.is_equal).then_inc(onehot_ready, 1)

            def mask_hidden(c):
                for a in range(HB):
                    dve.wait_ge(masks_projected, 3 * c + a + 2)
                    dve.wait_ge(gelu_done, 2 * c + a + 1)
                    dve.tensor_tensor(hid_m[:, c % 2, a, :], hid[:, c % 2, a, :], (S[2], S[3])[a][:, :],
                                      ALU.mult).then_inc(hid_masked, 1)

            def finish(c):
                dve.wait_ge(y_projected, c + 1)
                need(dve, y_stored[c % 2], 16 * (c // 2))
                dve.tensor_tensor(y_sb[:, c % 2, :, :], x2_tiles[:, 4 * c:4 * c + 4, :],
                                  PB[:, :].rearrange("p (s d) -> p s d", s=4), ALU.add).then_inc(y_ready, 1)

            norm_tiles(0)
            route(0)
            for c in range(T // 4):
                if c + 1 < T // 4:
                    norm_tiles(c + 1)
                mask_hidden(c)
                if c + 1 < T // 4:
                    route(c + 1)
                finish(c)

        @block.scalar
        def _(act):
            def step(G, b, g):
                if not live(G):
                    return
                slot = g % 2
                need(act, pv_done, G - 1)
                for k in range(BANKS):
                    act.wait_ge(max_ready, G * BANKS + k + 1)
                    for j in range(2):
                        hq, lb = k // 2, 2 * (k % 2) + j
                        i = hq * LB + lb
                        ins = act.activation(expd[:, slot, hq, lb, :], S[k % RING][:, j * N:(j + 1) * N], ACT.Exp,
                                             bias=neg_max[:, k, j:j + 1], scale=1.0,
                                             accum_out=row_sum[:, slot, i:i + 1])
                    ins.then_inc(exps_done, 1)

            schedule(act, step)
            act.wait_ge(hid_bias_ready, 1)
            for c in range(T // 4):
                need(act, hid_masked, 2 * (c - 1))
                act.wait_ge(masks_projected, 3 * c + 1)
                need(act, y_projected, c - 1)
                act.activation(mask_bf[:, c % 2, :], O[0:E, :], ACT.Copy).then_inc(mask_t_ready, 1)
                act.activation(mask_t[:, c % 2, :], O[0:E, :], ACT.Copy).then_inc(mask_t_ready, 1)
                for a in range(HB):
                    act.wait_ge(hid_projected, 2 * c + a + 1)
                    act.activation(hid[:, c % 2, a, :], S[a][:, :], ACT.Gelu, bias=hid_bias[:, a:a + 1],
                                   scale=1.0).then_inc(gelu_done, 1)

        @block.tensor
        def _(pe):
            def transpose(o, i):
                return pe.transpose(o, i, ident[:, :])

            pe.wait_ge(consts_ready, 9 + E)
            for i in range(4):
                pe.wait_ge(w_loaded, 16 * 4)
                transpose(M[:, i * D:(i + 1) * D], w_in[:, i, :]).then_inc(w_transposed, 1)

            def transpose_ctx(b):
                pe.wait_ge(ctx_loaded, 16 * (b + 1))
                need(pe, xn_t_ready, b)
                for k in range(LB):
                    ins = transpose(TB[:, k * P:(k + 1) * P], ctx_in[:, k, :])
                ins.then_inc(ctx_transposed, 1)

            def project_k(b):
                pe.wait_ge(ctx_t_ready, b + 1)
                need(pe, v_copied, b)
                pe.matmul(PB[:, :], w_t[:, 1, :], ctx_t[:, :], start=True, stop=True).then_inc(k_projected, 1)

            def transpose_xn(b):
                pe.wait_ge(xn_ready, b + 1)
                pe.wait_ge(ctx_t_ready, b + 1)
                for s in range(NB):
                    ins = transpose(TB[:, s * P:(s + 1) * P], xn[:, s, :])
                ins.then_inc(xn_transposed, 1)

            def project_q(b):
                pe.wait_ge(xn_t_ready, b + 1)
                pe.wait_ge(k_copied, b + 1)
                pe.matmul(PB[:, 0:N], w_t[:, 0, :], xn_t[:, :], start=True, stop=True).then_inc(q_projected, 1)

            def project_v(b):
                pe.wait_ge(q_copied, b + 1)
                for k in range(LB):
                    ins = pe.matmul(PB[:, k * P:(k + 1) * P], ctx_t[:, k * P:(k + 1) * P], w_t[:, 2, :],
                                    start=True, stop=True)
                ins.then_inc(v_projected, 1)

            transpose_ctx(0)
            pe.wait_ge(w_ready, 4)
            project_k(0)
            transpose_xn(0)
            project_q(0)

            def step(G, b, g):
                half0_of, half1_of = (half0_loaded, half1_loaded)
                for k in range(BANKS):
                    if live(G):
                        if k == 0 and g == 0:
                            pe.wait_ge(half0_of, (b + 1) * 16 * 12)
                        if k == 0 and g == GROUPS // 2:
                            pe.wait_ge(half1_of, (b + 1) * 16 * 12)
                        need(pe, exps_done, G * BANKS + k + 1 - RING)
                        h = GH * g + k // 2
                        for j in range(2):
                            lb = 2 * (k % 2) + j
                            ins = pe.matmul(S[k % RING][:, j * N:(j + 1) * N],
                                            k_stack[0:KROWS, h, lb * P:(lb + 1) * P],
                                            q_stack[0:KROWS, h, :], start=True, stop=True)
                        ins.then_inc(scores_ready, 1)
                    if k == 1 and live(G - 2):
                        pe.wait_ge(o_copied, G - 1)
                        need(pe, o_normed, G - 2)
                        if g == 2:
                            need(pe, x2_ready, b)
                        for s in range(NB):
                            ins = transpose(M[:, s * P:(s + 1) * P], o_sb[:, s * P:(s + 1) * P])
                        ins.then_inc(o_transposed, 1)
                    if g == 0 and live(G):
                        if k == 1:
                            project_v(b)
                        if stages_next(G):
                            if k == 3:
                                transpose_ctx(b + 1)
                            if k == 6:
                                project_k(b + 1)
                    if g == 1:
                        if stages_next(G):
                            if k == 0:
                                transpose_xn(b + 1)
                            if k == 4:
                                project_q(b + 1)
                        if live(G - 2) and (not isinstance(G, int) or G >= GROUPS):
                            if k == 3:
                                pe.wait_ge(o_normed, G - 1)
                                if not isinstance(b, int) or b > 1:
                                    pe.wait_ge(wo_projected, b - 1)
                                for s in range(NB):
                                    ins = transpose(M[:, s * P:(s + 1) * P], o_n[:, s, :])
                                ins.then_inc(o_t_transposed, 1)
                            if k == 5:
                                pe.wait_ge(o_t_copied, b)
                                for s in range(NB):
                                    ins = pe.matmul(M[:, s * P:(s + 1) * P], o_t[:, s * P:(s + 1) * P], w_t[:, 3, :],
                                                    start=True, stop=True)
                                ins.then_inc(wo_projected, 1)
                    if k >= BANKS - LB and live(G - 1):
                        lb = k - (BANKS - LB)
                        slot = (g - 1) % 2
                        if lb == 0:
                            pe.wait_ge(v_hat_ready, G)
                            need(pe, o_copied, G - 1)
                        for hq in range(GH):
                            ins = pe.matmul(O[32 * hq:32 * hq + 32, 0:N], v_hat[:, slot, hq, lb, :],
                                            expd[:, slot, hq, lb, :], start=(lb == 0), stop=(lb == LB - 1),
                                            tile_position=(0, 32 * hq))
                        if lb == LB - 1:
                            ins.then_inc(pv_done, 1)

            schedule(pe, step)

            pe.wait_ge(small_loaded, 7 * 16)
            for a in range(HB):
                ins = pe.matmul(TB[:, a * E:(a + 1) * E],
                                w1_raw[:, a * (E // HB):(a + 1) * (E // HB), :].rearrange("p e h -> p (e h)"),
                                bias_t[:, :], start=True, stop=True)
            ins.then_inc(bias_projected, 1)
            pe.wait_ge(bias_masked, 1)
            pe.wait_ge(w1_scaled, 1)
            pe.wait_ge(x2_ready, B)
            pe.wait_ge(exps_done, LASTG * BANKS)
            pe.wait_ge(o_copied, LASTG)

            def hidden(c):
                pe.wait_ge(xh_ready, c + 1)
                need(pe, xh_t_ready, c)
                for s in range(4):
                    ins = transpose(TB[:, s * P:(s + 1) * P], xh[:, s, :])
                ins.then_inc(xh_transposed, 1)
                pe.wait_ge(xh_t_ready, c + 1)
                need(pe, logits_copied, c)
                for s in range(4):
                    ins = pe.matmul(M[:, s * E:(s + 1) * E], xh_t[:, c % 2, s * P:(s + 1) * P], wg_t[:, :],
                                    start=True, stop=True)
                ins.then_inc(logits_projected, 1)
                need(pe, gelu_done, 2 * c)
                for a in range(HB):
                    w1_a = w1_s[:, a * (E // HB):(a + 1) * (E // HB), :].rearrange("p e h -> p (e h)")
                    pe.matmul(S[a][:, :], w1_a, xh_t[:, c % 2, :], start=True, stop=True).then_inc(hid_projected, 1)

            def masks(c):
                pe.wait_ge(onehot_ready, c + 1)
                need(pe, hid_masked, 2 * c)
                need(pe, mask_t_ready, 2 * c)
                for s in range(4):
                    ins = pe.matmul(O[0:E, s * P:(s + 1) * P], onehot[:, s, :], ident_bf[:, :], start=True, stop=True)
                ins.then_inc(masks_projected, 1)
                pe.wait_ge(mask_t_ready, 2 * c + 1)
                for a in range(HB):
                    pe.matmul((S[2], S[3])[a][:, :], expand[:, a, :], mask_bf[:, c % 2, :],
                              start=True, stop=True).then_inc(masks_projected, 1)

            def down(c):
                pe.wait_ge(hid_masked, 2 * (c + 1))
                pe.wait_ge(mask_t_ready, 2 * (c + 1))
                need(pe, y_ready, c)
                for s in range(4):
                    o = PB[:, s * D:(s + 1) * D]
                    for a in range(HB):
                        pe.matmul(o, hid_m[:, c % 2, a, s * P:(s + 1) * P], w2_sb[:, a, :], start=(a == 0), stop=False)
                    ins = pe.matmul(o, mask_t[:, c % 2, s * P:(s + 1) * P], b2_sb[:, :], start=False, stop=True)
                ins.then_inc(y_projected, 1)

            hidden(0)
            for c in range(T // 4):
                masks(c)
                if c + 1 < T // 4:
                    hidden(c + 1)
                down(c)


_INS = ["x", "ctx_1024", "L0_xattn_Wq", "L0_xattn_Wk", "L0_xattn_Wv", "L0_xattn_Wo", "L0_ffn_Wg",
        "L0_ffn_ln_scale", "L0_ffn_ln_bias", "L0_ffn_W1", "L0_ffn_b1", "L0_ffn_W2", "L0_ffn_b2"]


def kernel(**inputs):
    import numpy as _np
    import concourse.bacc as _bacc
    from concourse import mybir as _mybir
    from concourse.bass_utils import run_bass_kernel_spmd as _run

    nc = _bacc.Bacc("TRN2", target_bir_lowering=False, num_devices=1)
    arrays, args = {}, []
    for name in _INS:
        a = _np.ascontiguousarray(inputs[name])
        arrays[f"in_{name}"] = a
        args.append(nc.dram_tensor(f"in_{name}", a.shape, _mybir.dt.from_np(a.dtype), kind="ExternalInput").ap())
    x = arrays["in_x"]
    args.append(nc.dram_tensor("out_0", x.shape, _mybir.dt.from_np(x.dtype), kind="ExternalOutput").ap())
    cross_attention_moe(nc, *args)
    r = _run(nc, [arrays], core_ids=[0])
    return r.results[0]["out_0"]
```

```python
import concourse.bass as bass
from concourse import mybir
from contextlib import ExitStack

F32 = mybir.dt.float32
BF16 = mybir.dt.bfloat16
ALU = mybir.AluOpType
ACT = mybir.ActivationFunctionType
AX = mybir.AxisListType

P = 128
HEADS = 16
LN_EPS = 1e-5
PARTS = 3
GH = 4
DVE_BANKS = 4


def cross_attention_moe(nc, x, ctx, Wq, Wk, Wv, Wo, Wg, ln_scale, ln_bias, W1, b1, W2, b2, out):
    B, N, D = x.shape
    L = ctx.shape[1]
    C = D // HEADS
    NB, LB = N // P, L // P
    GROUPS = HEADS // GH
    BANKS = GH * LB // 2
    KROWS = PARTS * PARTS * C
    TERM = PARTS * C
    E, H = b1.shape
    EH = E * H
    HB = EH // P
    T = B * NB
    CHUNKS = T // 4
    SMALL = 4
    SCALE = float(D) ** -0.5
    RING = DVE_BANKS
    LASTG = B * GROUPS
    HALF = HEADS // 2
    LOADS = 2

    k_parts_dram = nc.dram_tensor("k_parts_dram", [PARTS, P, L], BF16, kind="Internal").ap()
    q_parts_dram = nc.dram_tensor("q_parts_dram", [PARTS, PARTS, P, N], BF16, kind="Internal").ap()

    with ExitStack() as stack:
        def sb(name, shape, dt=F32):
            return stack.enter_context(nc.sbuf_tensor(name, shape, dt))

        def bank(name):
            return stack.enter_context(nc.psum_tensor(name, [P, 512], F32))

        def sem(name):
            return stack.enter_context(nc.semaphore(name))

        ident = sb("ident", [P, P])
        ident_bf = sb("ident_bf", [P, P], BF16)
        w_in = sb("w_in", [P, 4, D])
        w_t = sb("w_t", [P, 4, D])
        x_all = sb("x_all", [P, B, NB, D])
        x2_all = sb("x2_all", [P, B, NB, D])
        ctx_in = sb("ctx_in", [P, LB, D])
        ctx_t = sb("ctx_t", [P, L])
        stats = sb("stats", [P, NB, 6])
        mean_var = sb("mean_var", [P, NB, 2])
        rstd = sb("rstd", [P, NB])
        minus_half = sb("minus_half", [P, T])
        eps = sb("eps", [P, NB])
        zero = sb("zero", [P, 1])
        xm = sb("xm", [P, NB, D])
        warm = sb("warm", [P, 1])
        xn = sb("xn", [P, NB, D])
        xn_t = sb("xn_t", [P, N])
        kf = sb("kf", [P, L])
        qf = sb("qf", [P, N])
        k_rest = sb("k_rest", [P, L])
        q_rest = sb("q_rest", [P, N])
        k_parts = sb("k_parts", [P, PARTS, L], BF16)
        q_parts = sb("q_parts", [P, PARTS, N], BF16)
        k_stack = sb("k_stack", [P, HEADS, L], BF16)
        q_stack = sb("q_stack", [P, HEADS, N], BF16)
        v_ones = sb("v_ones", [P, LB, HEADS, C + 1])
        v_hat = sb("v_hat", [P, GROUPS, GH, LB, 32])
        neg_max = sb("neg_max", [P, BANKS, 2])
        row_sum = sb("row_sum", [P, GROUPS, GH * LB])
        recip_sum = sb("recip_sum", [P, GROUPS, GH * LB])
        expd = sb("expd", [P, GROUPS, GH, LB, N])
        o_sb = sb("o_sb", [P, N])
        recip_den = sb("recip_den", [P, NB, GH])
        o_n = sb("o_n", [P, NB, D])
        o_t = sb("o_t", [P, N])

        wg_t = sb("wg_t", [P, E])
        scale_t = sb("scale_t", [P, E])
        bias_t = sb("bias_t", [P, E])
        w1_raw = sb("w1_raw", [P, E, H])
        w1_s = sb("w1_s", [P, E, H])
        b1_col = sb("b1_col", [P, HB])
        w2_sb = sb("w2_sb", [P, HB, D])
        b2_sb = sb("b2_sb", [E, D])
        b2_rest = sb("b2_rest", [E, D])
        b2_split = sb("b2_split", [E, PARTS, D], BF16)
        b2_parts = sb("b2_parts", [PARTS * E, D], BF16)
        own = sb("own", [P, HB, E])
        ones_e = sb("ones_e", [P, HB, E])
        own_bias = sb("own_bias", [P, HB, E])
        bias_sum = sb("bias_sum", [P, HB])
        hid_bias = sb("hid_bias", [P, HB])
        xh = sb("xh", [P, B, NB, D])
        xh_t = sb("xh_t", [P, CHUNKS, 512])
        logits = sb("logits", [P, 4, E])
        top = sb("top", [P, 4])
        first = sb("first", [P, 4, E])
        ftop = sb("ftop", [P, 4])
        order = sb("order", [P, E])
        onehot = sb("onehot", [P, CHUNKS, 4, PARTS, E], BF16)
        hid = sb("hid", [P, 2, HB, 512])
        hid_m = sb("hid_m", [P, 2, HB, 512])
        mask_bf = sb("mask_bf", [PARTS * E, 2, 512], BF16)
        expand = sb("expand", [E, HB, P], BF16)
        stats2 = sb("stats2", [P, NB, 6])
        mean_var2 = sb("mean_var2", [P, NB, 2])
        f_tmp = sb("f_tmp", [P, SMALL, NB])
        x2m = sb("x2m", [P, NB, D])
        y_sb = sb("y_sb", [P, 2, 4, D])

        S = [bank(f"scores{i}") for i in range(RING)]
        O = bank("o_acc")
        TB = bank("transposes")
        PB = bank("projections")
        M = bank("mixed")

        (consts_ready, ident_ready, filled, v_filled, ffn_consts, stats2_done, moments2_ready, w_qk_loaded, w_vo_loaded, x0_loaded, x_rest_loaded, ctx_loaded, small_loaded, w_transposed,
         w_ready, stats_done, moments_ready, eps_added, rstd_ready, mean_taken, xn_ready, xn_transposed, xn_t_ready,
         ctx_transposed, ctx_t_ready, k_projected, k_copied, q_projected, q_copied, v_projected, v_copied,
         k_split, q_split, k_parts_ready, q_parts_ready, k_stored, q_stored, half0_loaded, half1_loaded,
         scores_ready, max_ready, exps_done, recip_ready, v_hat_ready, pv_done, o_copied, o_transposed,
         den_ready, o_normed, o_t_transposed, o_t_copied, wo_projected, x2_ready) = [
            sem(n) for n in (
                "consts_ready ident_ready filled v_filled ffn_consts stats2_done moments2_ready w_qk_loaded w_vo_loaded x0_loaded x_rest_loaded ctx_loaded small_loaded w_transposed "
                "w_ready stats_done moments_ready eps_added rstd_ready mean_taken xn_ready xn_transposed xn_t_ready "
                "ctx_transposed ctx_t_ready k_projected k_copied q_projected q_copied v_projected v_copied "
                "k_split q_split k_parts_ready q_parts_ready k_stored q_stored half0_loaded half1_loaded "
                "scores_ready max_ready exps_done recip_ready v_hat_ready pv_done o_copied o_transposed "
                "den_ready o_normed o_t_transposed o_t_copied wo_projected x2_ready").split()]
        (f_small, x2_centred, xh_ready, xh_transposed, xh_t_ready, hid_projected, gelu_done,
         logits_projected, logits_copied, top_done, first_done, ftop_done, onehot_ready, mask_transposed, masks_projected, mask_t_ready,
         hid_masked, y_projected, y_ready, y_stored0, y_stored1, w1_scaled, bias_projected, bias_masked, bias_summed,
         hid_bias_ready, b2_stage, b2_split_ready, b2_parts_loaded) = [
            sem(n) for n in (
                "f_small x2_centred xh_ready xh_transposed xh_t_ready hid_projected gelu_done "
                "logits_projected logits_copied top_done first_done ftop_done onehot_ready mask_transposed masks_projected mask_t_ready "
                "hid_masked y_projected y_ready y_stored0 y_stored1 w1_scaled bias_projected bias_masked bias_summed "
                "hid_bias_ready b2_stage b2_split_ready b2_parts_loaded").split()]

        half_loaded = (half0_loaded, half1_loaded)
        y_stored = (y_stored0, y_stored1)

        def need(eng, semaphore, value):
            if not isinstance(value, int) or value > 0:
                eng.wait_ge(semaphore, value)

        AHEAD = 3
        PV_AT = ((1, 6), (2, 0), (2, 1), (2, 3))
        LOOPS = B - 2

        def schedule(eng, step, before=None):
            for G in range(AHEAD):
                if G == 2 and before is not None:
                    before()
                step(G, 0, G)
            with eng.Fori(0, LOOPS) as r:
                for i in range(AHEAD, AHEAD + GROUPS):
                    step(r * GROUPS + i, r + i // GROUPS, i % GROUPS)
            for G in range(LOOPS * GROUPS + AHEAD, LASTG + AHEAD):
                step(G, G // GROUPS, G % GROUPS)

        def stages_next(G):
            return not isinstance(G, int) or G // GROUPS + 1 < B

        def norms_ahead(G):
            return not isinstance(G, int) or G // GROUPS + 2 < B

        def finishes(G):
            return not isinstance(G, int) or G >= GROUPS

        def live(G):
            return not isinstance(G, int) or 0 <= G < LASTG

        def split(eng, full, rest, parts, stage_done, ready, b):
            zeros = zero[0:full.shape[0], :].to_broadcast([full.shape[0], full.shape[1]])
            eng.tensor_tensor(parts[:, 0, :], full[:, :], zeros, ALU.add).then_inc(stage_done, 1)
            eng.wait_ge(stage_done, 3 * b + 1)
            eng.tensor_tensor(rest[:, :], full[:, :], parts[:, 0, :], ALU.subtract).then_inc(stage_done, 1)
            eng.wait_ge(stage_done, 3 * b + 2)
            eng.tensor_tensor(parts[:, 1, :], rest[:, :], zeros, ALU.add).then_inc(stage_done, 1)
            eng.wait_ge(stage_done, 3 * b + 3)
            eng.tensor_tensor(parts[:, 2, :], rest[:, :], parts[:, 1, :], ALU.subtract).then_inc(ready, 1)

        block = stack.enter_context(nc.Block())

        @block.sync
        def _(sp):
            def load_ctx(b):
                sp.dma_start(ctx_in[:, :, :], ctx[b].rearrange("(k p) d -> p k d", p=P)).then_inc(ctx_loaded, 16)

            def heads_of(half):
                return slice(half * HALF, (half + 1) * HALF)

            def load_k(half):
                kd = k_parts_dram.rearrange("b (c h) l -> (b c) h l", h=HEADS)[:, heads_of(half), :]
                sp.dma_start(k_stack[0:KROWS, heads_of(half), :], kd.unsqueeze(0).to_broadcast([PARTS, TERM, HALF, L])).then_inc(half_loaded[half], 16)

            def load_q(half):
                qd = q_parts_dram.rearrange("a b (c h) n -> (a b c) h n", h=HEADS)[:, heads_of(half), :]
                sp.dma_start(q_stack[0:KROWS, heads_of(half), :], qd).then_inc(half_loaded[half], 16)

            def store_k(b, wait=True):
                sp.wait_ge(k_parts_ready, b + 1)
                sp.dma_start(k_parts_dram.rearrange("b p l -> p b l"), k_parts[:, :, :]).then_inc(k_stored, 16)
                if wait:
                    sp.wait_ge(k_stored, (b + 1) * 16)

            def store_q_copy(b, t):
                sp.wait_ge(q_parts_ready, b + 1)
                sp.dma_start(q_parts_dram[:, t].rearrange("a p n -> p a n"), q_parts[:, :, :]).then_inc(q_stored, 16)

            def store_q(b):
                for t in range(PARTS):
                    store_q_copy(b, t)
                sp.wait_ge(q_stored, (b + 1) * 16 * PARTS)

            sp.dma_start(x_all[:, 0, :, :], x[0].rearrange("(s p) d -> p s d", p=P)).then_inc(x0_loaded, 16)
            for i, w in enumerate((Wq, Wk)):
                sp.dma_start(w_in[:, i, :], w).then_inc(w_qk_loaded, 16)
            load_ctx(0)
            for i, w in enumerate((Wv, Wo)):
                sp.dma_start(w_in[:, 2 + i, :], w).then_inc(w_vo_loaded, 16)
            for b in range(1, B):
                sp.dma_start(x_all[:, b, :, :], x[b].rearrange("(s p) d -> p s d", p=P)).then_inc(x_rest_loaded, 16)
            sp.wait_ge(ctx_transposed, 1)
            load_ctx(1)
            store_k(0, wait=False)
            for t in range(PARTS):
                store_q_copy(0, t)
            sp.wait_ge(k_stored, 16)
            load_k(0)
            sp.wait_ge(q_stored, 16 * PARTS)
            load_q(0)
            load_k(1)
            load_q(1)
            with nc.allow_non_contiguous_dma(reason="small weights"):
                sp.dma_start(wg_t[:, :], Wg.rearrange("e d -> d e")).then_inc(small_loaded, 16)
                sp.dma_start(scale_t[:, :], ln_scale.rearrange("e d -> d e")).then_inc(small_loaded, 16)
                sp.dma_start(bias_t[:, :], ln_bias.rearrange("e d -> d e")).then_inc(small_loaded, 16)
                sp.dma_start(w1_raw[:, :, :], W1.rearrange("e d h -> d e h")).then_inc(small_loaded, 16)
                sp.dma_start(b1_col[:, :], b1.rearrange("(a e) h -> (e h) a", a=HB)).then_inc(small_loaded, 16)
            sp.dma_start(w2_sb[:, :, :], W2.rearrange("(a e) h d -> (e h) a d", a=HB)).then_inc(small_loaded, 16)
            sp.dma_start(b2_sb[:, :], b2).then_inc(small_loaded, 16)

            def batch(b, more):
                if more:
                    sp.wait_ge(ctx_transposed, b + 2)
                    load_ctx(b + 2)
                sp.wait_ge(half1_loaded, (b + 1) * 16 * LOADS)
                store_k(b + 1)
                sp.wait_ge(scores_ready, (b * GROUPS + 2) * BANKS)
                load_k(0)
                store_q(b + 1)
                load_q(0)
                sp.wait_ge(scores_ready, (b * GROUPS + 4) * BANKS)
                load_k(1)
                load_q(1)

            with sp.Fori(0, B - 2) as b:
                batch(b, True)
            batch(B - 2, False)
            sp.wait_ge(b2_split_ready, 1)
            for a in range(PARTS):
                sp.dma_start(b2_parts[a * E:(a + 1) * E, :], b2_split[:, a, :]).then_inc(b2_parts_loaded, 16)
            for c in range(CHUNKS):
                sp.wait_ge(y_ready, c + 1)
                sp.dma_start(out[2 * c:2 * c + 2].rearrange("b (s p) d -> p (b s) d", p=P),
                             y_sb[:, c % 2, :, :]).then_inc(y_stored[c % 2], 16)
            for stored in y_stored:
                sp.wait_ge(stored, 16 * (T // 8))

        @block.gpsimd
        def _(pool):
            for m in (ident, ident_bf):
                pool.memset(m[:, :], 0.0).then_inc(filled, 1)
            pool.wait_ge(filled, 2)
            for m in (ident, ident_bf):
                pool.affine_select(out=m[:, :], in_=m[:, :], compare_op=ALU.not_equal, fill=1.0, base=0,
                                   pattern=[[-1, P]], channel_multiplier=1).then_inc(ident_ready, 1)
            pool.memset(minus_half[:, :], -0.5).then_inc(consts_ready, 1)
            pool.memset(eps[:, :], LN_EPS).then_inc(consts_ready, 1)
            pool.memset(zero[:, :], 0.0).then_inc(consts_ready, 1)
            pool.wait_ge(consts_ready, 3)

            def make_rstd(b):
                pool.wait_ge(moments_ready, 2 * (b + 1))
                need(pool, xn_ready, b)
                pool.tensor_tensor(rstd[:, :], mean_var[:, :, 1], eps[:, :], ALU.add).then_inc(eps_added, 1)
                pool.wait_ge(eps_added, b + 1)
                pool.tensor_tensor(rstd[:, :], rstd[:, :], minus_half[:, 0:NB], ALU.pow).then_inc(rstd_ready, 1)

            def split_k(b):
                pool.wait_ge(k_copied, b + 1)
                need(pool, k_stored, 16 * b)
                split(pool, kf, k_rest, k_parts, k_split, k_parts_ready, b)

            def split_q(b):
                pool.wait_ge(q_copied, b + 1)
                need(pool, q_stored, 16 * PARTS * b)
                split(pool, qf, q_rest, q_parts, q_split, q_parts_ready, b)

            def make_v_hat(G, b, g):
                pool.wait_ge(recip_ready, G + 1)
                pool.wait_ge(v_copied, b + 1)
                slot = g
                pool.tensor_tensor(
                    v_hat[:, slot, :, :, 0:C + 1],
                    v_ones[:, :, GH * g:GH * g + GH, :].rearrange("p l h c -> p h l c"),
                    recip_sum[:, slot, :].rearrange("p (h l) -> p h l", h=GH).unsqueeze(3)
                    .to_broadcast([P, GH, LB, C + 1]),
                    ALU.mult).then_inc(v_hat_ready, 1)

            def x_norm(b):
                pool.tensor_tensor(xm[:, :, :], x_all[:, b, :, :],
                                   mean_var[:, :, 0:1].to_broadcast([P, NB, D]), ALU.subtract).then_inc(mean_taken, 1)
                pool.wait_ge(mean_taken, b - 1)
                pool.tensor_tensor(xn[:, :, :], xm[:, :, :], rstd[:, :].unsqueeze(2).to_broadcast([P, NB, D]),
                                   ALU.mult).then_inc(xn_ready, 1)

            make_rstd(0)
            pool.memset(v_ones[:, :, :, :], 1.0).then_inc(v_filled, 1)
            split_q(0)
            make_rstd(1)
            pool.memset(v_hat[:, :, :, :, :], 0.0).then_inc(v_filled, 1)
            for e in range(E):
                pool.memset(order[:, e:e + 1], float(E - e)).then_inc(ffn_consts, 1)
            pool.memset(own[:, :, :], 1.0).then_inc(filled, 1)
            pool.memset(expand[:, :, :], 1.0).then_inc(filled, 1)
            pool.wait_ge(filled, 4)
            pool.affine_select(out=own[:, :, :], in_=own[:, :, :], compare_op=ALU.is_ge, fill=0.0, base=0,
                               pattern=[[P, HB], [-H, E]], channel_multiplier=1).then_inc(filled, 1)
            pool.affine_select(out=expand[:, :, :], in_=expand[:, :, :], compare_op=ALU.is_ge, fill=0.0, base=0,
                               pattern=[[P, HB], [1, P]], channel_multiplier=-H).then_inc(filled, 1)
            pool.wait_ge(filled, 6)
            pool.affine_select(out=own[:, :, :], in_=own[:, :, :], compare_op=ALU.is_ge, fill=0.0, base=H - 1,
                               pattern=[[-P, HB], [H, E]], channel_multiplier=-1).then_inc(ffn_consts, 1)
            pool.affine_select(out=expand[:, :, :], in_=expand[:, :, :], compare_op=ALU.is_ge, fill=0.0, base=H - 1,
                               pattern=[[-P, HB], [-1, P]], channel_multiplier=H).then_inc(ffn_consts, 1)
            pool.wait_ge(v_filled, 2)

            def ffn_norm(b):
                mean, var = mean_var2[:, :, 0:1], mean_var2[:, :, 1]
                pool.wait_ge(moments2_ready, 2 * (b + 1))
                half = minus_half[:, 0:NB]
                done = b * SMALL

                def chained(out, in0, in1, op):
                    nonlocal done
                    done = done + 1
                    pool.tensor_tensor(out, in0, in1, op).then_inc(f_small, 1)
                    pool.wait_ge(f_small, done)

                chained(f_tmp[:, 0, :], var, eps[:, :], ALU.add)
                chained(f_tmp[:, 1, :], f_tmp[:, 0, :], eps[:, :], ALU.mult)
                chained(f_tmp[:, 2, :], f_tmp[:, 1, :], var, ALU.add)
                chained(f_tmp[:, 3, :], f_tmp[:, 2, :], half, ALU.pow)
                pool.tensor_tensor(x2m[:, :, :], x2_all[:, b, :, :], mean.to_broadcast([P, NB, D]),
                                   ALU.subtract).then_inc(x2_centred, 1)
                pool.wait_ge(x2_centred, b + 1)
                pool.tensor_tensor(xh[:, b, :, :], x2m[:, :, :],
                                   f_tmp[:, 3, :].unsqueeze(2).to_broadcast([P, NB, D]), ALU.mult).then_inc(xh_ready, 1)

            def step(G, b, g):
                if live(G - 1):
                    make_v_hat(G - 1, b - 1 if g == 0 else b, (g - 1) % GROUPS)
                if g == 1 and stages_next(G):
                    split_k(b + 1)
                if g == 2:
                    if stages_next(G):
                        split_q(b + 1)
                    if finishes(G):
                        ffn_norm(b - 1)
                if g == 3 and norms_ahead(G):
                    pool.wait_ge(xn_transposed, b + 2)
                    make_rstd(b + 2)
                    x_norm(b + 2)

            def split_b2():
                pool.wait_ge(small_loaded, 7 * 16)
                split(pool, b2_sb, b2_rest, b2_split, b2_stage, b2_split_ready, 0)

            schedule(pool, step, split_b2)

        @block.vector
        def _(dve):
            def x_stats(b):
                if isinstance(b, int) and b == 0:
                    dve.wait_ge(x0_loaded, 16)
                else:
                    dve.wait_ge(x_rest_loaded, 16 * (B - 1))
                    dve.wait_ge(xn_ready, b)
                for s in range(NB):
                    dve.bn_stats(stats[:, s, :], x_all[:, b, s, :]).then_inc(stats_done, 1)

            def x_moments():
                for s in range(NB):
                    dve.bn_aggr(mean_var[:, s, :], stats[:, s, :]).then_inc(moments_ready, 1)

            def x_norm(b):
                dve.wait_ge(moments_ready, 2 * (b + 1))
                dve.wait_ge(rstd_ready, b + 1)
                need(dve, xn_transposed, b)
                for s in range(NB):
                    ins = dve.tensor_scalar(xn[:, s, :], x_all[:, b, s, :], mean_var[:, s, 0:1], rstd[:, s:s + 1],
                                            ALU.subtract, ALU.mult)
                ins.then_inc(xn_ready, 1)

            def copy_ctx_t(b):
                dve.wait_ge(ctx_transposed, b + 1)
                need(dve, v_projected, b)
                dve.tensor_copy(ctx_t[:, :], TB[:, :]).then_inc(ctx_t_ready, 1)

            def copy_k(b):
                dve.wait_ge(k_projected, b + 1)
                need(dve, k_parts_ready, b)
                dve.tensor_copy(kf[:, :], PB[:, :]).then_inc(k_copied, 1)

            def copy_xn_t(b):
                dve.wait_ge(xn_transposed, b + 1)
                need(dve, q_projected, b)
                dve.tensor_copy(xn_t[:, :], TB[:, 0:N]).then_inc(xn_t_ready, 1)

            def copy_q(b):
                dve.wait_ge(q_projected, b + 1)
                need(dve, q_parts_ready, b)
                dve.tensor_scalar(qf[:, :], PB[:, 0:N], SCALE, None, ALU.mult).then_inc(q_copied, 1)

            def copy_v(b):
                dve.wait_ge(v_projected, b + 1)
                need(dve, v_hat_ready, b * GROUPS)
                dve.tensor_copy(v_ones[:, :, :, 0:C],
                                PB[:, :].rearrange("p (l h c) -> p l h c", l=LB, h=HEADS)).then_inc(v_copied, 1)

            x_stats(0)
            dve.wait_ge(stats_done, NB)
            x_moments()
            x_norm(0)
            dve.wait_ge(xn_transposed, 1)
            dve.tensor_copy(xn_t[:, :], S[0][:, 0:N]).then_inc(xn_t_ready, 1)
            dve.wait_ge(consts_ready, 3)
            dve.wait_ge(k_copied, 1)
            split(dve, kf, k_rest, k_parts, k_split, k_parts_ready, 0)
            x_stats(1)
            dve.wait_ge(stats_done, 2 * NB)
            x_moments()
            x_norm(1)

            def step(G, b, g):
                for k in range(BANKS):
                    if live(G):
                        if g == 3 and k == 3 and norms_ahead(G):
                            dve.wait_ge(stats_done, (b + 3) * NB)
                        if g == 2 and k == 6 and finishes(G):
                            dve.wait_ge(x2_ready, b)
                            need(dve, xh_ready, b - 1)
                        if g == 2 and k == 7 and finishes(G):
                            dve.wait_ge(stats2_done, b * NB)
                        dve.wait_ge(scores_ready, G * BANKS + k + 1)
                        dve.tensor_reduce(neg_max[:, k, :], S[k % RING][:, :].rearrange("p (j n) -> p j n", j=2),
                                          AX.X, ALU.max, negate=True).then_inc(max_ready, 1)
                    if k == 4 and live(G - 2):
                        dve.wait_ge(pv_done, G - 1)
                        need(dve, o_transposed, G - 2)
                        dve.tensor_copy(o_sb[:, :], O[:, 0:N]).then_inc(o_copied, 1)
                    if k == 7 and live(G - 2):
                        g2 = (g - 2) % GROUPS
                        dve.wait_ge(o_transposed, G - 1)
                        o_view = M[:, 0:NB * P].rearrange("p (s h c) -> p s h c", s=NB, h=GH)
                        dve.reciprocal(recip_den[:, :, :], o_view[:, :, :, C]).then_inc(den_ready, 1)
                        dve.wait_ge(den_ready, G - 1)
                        if g2 == 0:
                            need(dve, o_t_transposed, b)
                        dve.tensor_tensor(
                            o_n[:, :, g2 * GH * C:(g2 + 1) * GH * C].rearrange("p s (h c) -> p s h c", h=GH),
                            o_view[:, :, :, 0:C],
                            recip_den[:, :, :].unsqueeze(3).to_broadcast([P, NB, GH, C]),
                            ALU.mult).then_inc(o_normed, 1)
                    if k == 3 and live(G - 1):
                        slot = (g - 1) % GROUPS
                        dve.wait_ge(exps_done, G * BANKS)
                        dve.reciprocal(recip_sum[:, slot, :], row_sum[:, slot, :]).then_inc(recip_ready, 1)
                    if g == 0 and live(G):
                        if k == 5:
                            copy_v(b)
                        if stages_next(G) and k == 7:
                            copy_ctx_t(b + 1)
                    if g == 3 and live(G) and norms_ahead(G):
                        if k == 1:
                            x_stats(b + 2)
                        if k == 4:
                            x_moments()
                    if g == 1 and stages_next(G):
                        if k == 3:
                            copy_xn_t(b + 1)
                        if k == 5:
                            copy_k(b + 1)
                    if g == 2 and k == 0 and stages_next(G):
                        copy_q(b + 1)
                    if g == 2 and finishes(G):
                            if k == 2:
                                dve.wait_ge(o_t_transposed, b)
                                dve.tensor_copy(o_t[:, :], TB[:, 0:N]).then_inc(o_t_copied, 1)
                            if k == 5:
                                dve.wait_ge(wo_projected, b)
                                dve.tensor_tensor(x2_all[:, b - 1, :, :], x_all[:, b - 1, :, :],
                                                  TB[:, 0:N].rearrange("p (s d) -> p s d", s=NB),
                                                  ALU.add).then_inc(x2_ready, 1)
                            if k == 6:
                                if not live(G):
                                    dve.wait_ge(x2_ready, b)
                                for s in range(NB):
                                    dve.bn_stats(stats2[:, s, :], x2_all[:, b - 1, s, :]).then_inc(stats2_done, 1)
                            if k == 7:
                                if not live(G):
                                    dve.wait_ge(stats2_done, b * NB)
                                for s in range(NB):
                                    dve.bn_aggr(mean_var2[:, s, :], stats2[:, s, :]).then_inc(moments2_ready, 1)
                    if isinstance(G, int):
                        ffn_step(G, k)

            def ffn_weights():
                dve.wait_ge(small_loaded, 7 * 16)
                dve.wait_ge(ffn_consts, E + 2)
                dve.tensor_tensor(w1_s[:, :, :], w1_raw[:, :, :], scale_t[:, :].unsqueeze(2).to_broadcast([P, E, H]),
                                  ALU.mult).then_inc(w1_scaled, 1)
                dve.wait_ge(bias_projected, 1)
                dve.tensor_tensor(own_bias[:, :, :], own[:, :, :],
                                  M[:, 0:HB * E].rearrange("p (a e) -> p a e", a=HB), ALU.mult).then_inc(bias_masked, 1)
                dve.wait_ge(bias_masked, 1)
                dve.tensor_reduce(bias_sum[:, :], own_bias[:, :, :], AX.X, ALU.add).then_inc(bias_summed, 1)
                dve.wait_ge(bias_summed, 1)
                dve.tensor_tensor(hid_bias[:, :], bias_sum[:, :], b1_col[:, :], ALU.add).then_inc(hid_bias_ready, 1)

            x2_tiles = x2_all[:, :, :, :].rearrange("p b s d -> p (b s) d")

            def copy_xh_t(c):
                dve.wait_ge(xh_transposed, c + 1)
                dve.tensor_copy(xh_t[:, c, :], TB[:, :]).then_inc(xh_t_ready, 1)

            def route(c):
                dve.wait_ge(logits_projected, c + 1)
                dve.tensor_copy(logits[:, :, :], PB[:, 0:4 * E].rearrange("p (s e) -> p s e", s=4)).then_inc(logits_copied, 1)
                dve.wait_ge(logits_copied, c + 1)
                dve.tensor_reduce(top[:, :], logits[:, :, :], AX.X, ALU.max).then_inc(top_done, 1)
                dve.wait_ge(top_done, c + 1)
                dve.tensor_tensor(first[:, :, :], logits[:, :, :], top[:, :].unsqueeze(2).to_broadcast([P, 4, E]),
                                  ALU.is_equal).then_inc(first_done, 1)
                dve.wait_ge(first_done, 2 * c + 1)
                dve.tensor_tensor(first[:, :, :], first[:, :, :], order[:, :].unsqueeze(1).to_broadcast([P, 4, E]),
                                  ALU.mult).then_inc(first_done, 1)
                dve.wait_ge(first_done, 2 * c + 2)
                dve.tensor_reduce(ftop[:, :], first[:, :, :], AX.X, ALU.max).then_inc(ftop_done, 1)
                dve.wait_ge(ftop_done, c + 1)
                dve.tensor_tensor(onehot[:, c, :, :, :],
                                  first[:, :, :].unsqueeze(2).to_broadcast([P, 4, PARTS, E]),
                                  ftop[:, :].unsqueeze(2).unsqueeze(3).to_broadcast([P, 4, PARTS, E]),
                                  ALU.is_equal).then_inc(onehot_ready, 1)

            def mask_hidden(c):
                for a in range(HB):
                    dve.wait_ge(masks_projected, HB * c + a + 1)
                    dve.wait_ge(gelu_done, HB * c + a + 1)
                    need(dve, y_projected, c - 1)
                    dve.tensor_tensor(hid_m[:, c % 2, a, :], hid[:, c % 2, a, :], S[2 + a][:, :],
                                      ALU.mult).then_inc(hid_masked, 1)

            def finish(c):
                dve.wait_ge(y_projected, c + 1)
                need(dve, y_stored[c % 2], 16 * (c // 2))
                dve.tensor_tensor(y_sb[:, c % 2, :, :], x2_tiles[:, 4 * c:4 * c + 4, :],
                                  PB[:, :].rearrange("p (s d) -> p s d", s=4), ALU.add).then_inc(y_ready, 1)

            def ffn_step(G, k):
                if (G, k) == (LASTG - 4, 7):
                    copy_xh_t(0)
                if (G, k) == (LASTG - 3, 3):
                    route(0)
                if (G, k) == (LASTG - 3, 5):
                    copy_xh_t(1)
                if (G, k) == (LASTG - 2, 1):
                    route(1)
                if (G, k) == (LASTG - 1, 0):
                    copy_xh_t(2)
                if (G, k) == (LASTG - 1, 4):
                    route(2)
                if (G, k) == (LASTG + 1, 6):
                    mask_hidden(0)
                if (G, k) == (LASTG + 2, 1):
                    finish(0)
                if (G, k) == (LASTG + 2, 3):
                    mask_hidden(1)

            schedule(dve, step, ffn_weights)
            finish(1)
            mask_hidden(2)
            copy_xh_t(3)
            route(3)
            finish(2)
            mask_hidden(3)
            finish(3)

        @block.scalar
        def _(act):
            def step(G, b, g):
                if not live(G):
                    return
                slot = g
                for k in range(BANKS):
                    act.wait_ge(max_ready, G * BANKS + k + 1)
                    for j in range(2):
                        hq, lb = k // 2, 2 * (k % 2) + j
                        i = hq * LB + lb
                        ins = act.activation(expd[:, slot, hq, lb, :], S[k % RING][:, j * N:(j + 1) * N], ACT.Exp,
                                             bias=neg_max[:, k, j:j + 1], scale=1.0,
                                             accum_out=row_sum[:, slot, i:i + 1])
                    ins.then_inc(exps_done, 1)

            def copy_weight(i, bank_, place):
                act.wait_ge(w_transposed, i + 1)
                src = bank_[:, place * D:(place + 1) * D]
                dst = w_t[:, i, :]
                if i < 2:
                    src = src.rearrange("p (h c) -> p h c", h=HEADS)
                    dst = dst.rearrange("p (c h) -> p h c", h=HEADS)
                act.activation(dst, src, ACT.Copy).then_inc(w_ready, 1)

            act.wait_ge(consts_ready, 3)
            act.activation(warm[:, :], zero[:, :], ACT.Exp)
            act.wait_ge(w_transposed, 2)
            copy_weight(0, M, 0)
            copy_weight(1, M, 1)
            act.wait_ge(ctx_transposed, 1)
            act.activation(ctx_t[:, :], TB[:, :], ACT.Copy).then_inc(ctx_t_ready, 1)
            act.wait_ge(k_projected, 1)
            act.activation(kf[:, :], PB[:, :], ACT.Copy).then_inc(k_copied, 1)
            act.wait_ge(q_projected, 1)
            act.activation(qf[:, :], S[1][:, 0:N], ACT.Copy, scale=SCALE).then_inc(q_copied, 1)
            act.wait_ge(w_transposed, 4)
            copy_weight(2, S[3], 0)
            copy_weight(3, S[3], 1)

            schedule(act, step)

            def copy_mask(c):
                act.wait_ge(mask_transposed, c + 1)
                need(act, y_projected, c - 1)
                act.activation(mask_bf[:, c % 2, :], TB[0:PARTS * E, :], ACT.Copy).then_inc(mask_t_ready, 1)

            def gelu(c):
                need(act, hid_masked, HB * (c - 1))
                for a in range(HB):
                    act.wait_ge(hid_projected, HB * c + a + 1)
                    act.activation(hid[:, c % 2, a, :], S[a][:, :], ACT.Gelu, bias=hid_bias[:, a:a + 1],
                                   scale=1.0).then_inc(gelu_done, 1)

            act.wait_ge(hid_bias_ready, 1)
            for c in range(CHUNKS - 1):
                copy_mask(c)
                gelu(c)
            gelu(3)
            copy_mask(3)

        @block.tensor
        def _(pe):
            def transpose(o, i):
                return pe.transpose(o, i, ident[:, :])

            def transpose_weight(i, bank_, place):
                transpose(bank_[:, place * D:(place + 1) * D], w_in[:, i, :]).then_inc(w_transposed, 1)

            def transpose_ctx(b):
                pe.wait_ge(ctx_loaded, 16 * (b + 1))
                need(pe, xn_t_ready, b)
                for k in range(LB):
                    ins = transpose(TB[:, k * P:(k + 1) * P], ctx_in[:, k, :])
                ins.then_inc(ctx_transposed, 1)

            def project_k(b, half):
                pe.wait_ge(ctx_t_ready, b + 1)
                need(pe, v_copied, b)
                cols = slice(half * L // 2, (half + 1) * L // 2)
                ins = pe.matmul(PB[:, cols], w_t[:, 1, :], ctx_t[:, cols], start=True, stop=True)
                if half == 1:
                    ins.then_inc(k_projected, 1)

            def transpose_xn(b):
                first = isinstance(b, int) and b == 0
                pe.wait_ge(xn_ready, b + 1)
                if not first:
                    pe.wait_ge(ctx_t_ready, b + 1)
                for s in range(NB):
                    ins = transpose((S[0] if first else TB)[:, s * P:(s + 1) * P], xn[:, s, :])
                ins.then_inc(xn_transposed, 1)

            def project_q(b):
                first = isinstance(b, int) and b == 0
                pe.wait_ge(xn_t_ready, b + 1)
                if not first:
                    pe.wait_ge(k_copied, b + 1)
                pe.matmul((S[1] if first else PB)[:, 0:N], w_t[:, 0, :], xn_t[:, :],
                          start=True, stop=True).then_inc(q_projected, 1)

            def project_v(b, half):
                pe.wait_ge(q_copied, b + 1)
                if isinstance(b, int) and b == 0:
                    pe.wait_ge(k_copied, 1)
                for k in range(half * LB // 2, (half + 1) * LB // 2):
                    ins = pe.matmul(PB[:, k * P:(k + 1) * P], ctx_t[:, k * P:(k + 1) * P], w_t[:, 2, :],
                                    start=True, stop=True)
                if half == 1:
                    ins.then_inc(v_projected, 1)

            pe.wait_ge(ident_ready, 2)
            pe.wait_ge(w_qk_loaded, 32)
            transpose_weight(0, M, 0)
            transpose_weight(1, M, 1)
            transpose_ctx(0)
            transpose_xn(0)
            pe.wait_ge(w_ready, 2)
            project_k(0, 0)
            project_k(0, 1)
            project_q(0)
            pe.wait_ge(w_vo_loaded, 32)
            transpose_weight(2, S[3], 0)
            transpose_weight(3, S[3], 1)
            pe.wait_ge(w_ready, 4)

            def step(G, b, g):
                for k in range(BANKS):
                    if live(G):
                        if k == 0 and g == 0:
                            pe.wait_ge(half0_loaded, (b + 1) * 16 * LOADS)
                        if k == 0 and g == GROUPS // 2:
                            pe.wait_ge(half1_loaded, (b + 1) * 16 * LOADS)
                        need(pe, exps_done, G * BANKS + k + 1 - RING)
                        h = GH * g + k // 2
                        for j in range(2):
                            lb = 2 * (k % 2) + j
                            ins = pe.matmul(S[k % RING][:, j * N:(j + 1) * N],
                                            k_stack[0:KROWS, h, lb * P:(lb + 1) * P],
                                            q_stack[0:KROWS, h, :], start=True, stop=True)
                        ins.then_inc(scores_ready, 1)
                    if k == 6 and live(G - 2):
                        pe.wait_ge(o_copied, G - 1)
                        need(pe, o_normed, G - 2)
                        for s in range(NB):
                            ins = transpose(M[:, s * P:(s + 1) * P], o_sb[:, s * P:(s + 1) * P])
                        ins.then_inc(o_transposed, 1)
                    if g == 0 and live(G):
                        if k == 2:
                            project_v(b, 0)
                        if k == 4:
                            project_v(b, 1)
                        if k == 5 and stages_next(G):
                            transpose_ctx(b + 1)
                    if g == 1 and stages_next(G):
                        if k == 1:
                            project_k(b + 1, 0)
                        if k == 2:
                            transpose_xn(b + 1)
                        if k == 4:
                            project_k(b + 1, 1)
                        if k == 7:
                            project_q(b + 1)
                    if g == 2 and finishes(G):
                        if k == 1:
                            pe.wait_ge(o_normed, G - 2)
                            for s in range(NB):
                                ins = transpose(TB[:, s * P:(s + 1) * P], o_n[:, s, :])
                            ins.then_inc(o_t_transposed, 1)
                        if k == 4:
                            pe.wait_ge(o_t_copied, b)
                            for s in range(NB):
                                ins = pe.matmul(TB[:, s * P:(s + 1) * P], o_t[:, s * P:(s + 1) * P], w_t[:, 3, :],
                                                start=True, stop=True)
                            ins.then_inc(wo_projected, 1)
                    for lb, (lag, at) in enumerate(PV_AT):
                        if at != k or not live(G - lag):
                            continue
                        slot = (g - lag) % GROUPS
                        if lb == 0:
                            pe.wait_ge(v_hat_ready, G)
                            need(pe, o_copied, G - 1)
                        for hq in range(GH):
                            ins = pe.matmul(O[32 * hq:32 * hq + 32, 0:N], v_hat[:, slot, hq, lb, :],
                                            expd[:, slot, hq, lb, :], start=(lb == 0), stop=(lb == LB - 1),
                                            tile_position=(0, 32 * hq))
                        if lb == LB - 1:
                            ins.then_inc(pv_done, 1)
                    if isinstance(G, int):
                        ffn_step(G, k)

            def ffn_weights():
                pe.wait_ge(small_loaded, 7 * 16)
                for a in range(HB):
                    ins = pe.matmul(M[:, a * E:(a + 1) * E],
                                    w1_raw[:, a * (E // HB):(a + 1) * (E // HB), :].rearrange("p e h -> p (e h)"),
                                    bias_t[:, :], start=True, stop=True)
                ins.then_inc(bias_projected, 1)
                pe.wait_ge(bias_masked, 1)

            def transpose_xh(c):
                pe.wait_ge(xh_ready, 2 * (c + 1))
                need(pe, xh_t_ready, c)
                if c == 2:
                    pe.wait_ge(x2_ready, B - 1)
                if c == 3:
                    pe.wait_ge(mask_t_ready, 3)
                for s in range(4):
                    ins = transpose(TB[:, s * P:(s + 1) * P], xh[:, (4 * c + s) // NB, (4 * c + s) % NB, :])
                ins.then_inc(xh_transposed, 1)

            def project_logits(c):
                pe.wait_ge(xh_t_ready, c + 1)
                need(pe, logits_copied, c)
                if c == 0:
                    pe.wait_ge(v_copied, B)
                if c == 3:
                    pe.wait_ge(y_ready, 2)
                for s in range(4):
                    ins = pe.matmul(PB[:, s * E:(s + 1) * E], xh_t[:, c, s * P:(s + 1) * P], wg_t[:, :],
                                    start=True, stop=True)
                ins.then_inc(logits_projected, 1)

            def hidden(c):
                pe.wait_ge(xh_t_ready, c + 1)
                if c == 0:
                    pe.wait_ge(w1_scaled, 1)
                for a in range(HB):
                    if c == 0:
                        pe.wait_ge(exps_done, LASTG * BANKS - RING + a + 1)
                    need(pe, gelu_done, HB * (c - 1) + a + 1)
                    w1_a = w1_s[:, a * (E // HB):(a + 1) * (E // HB), :].rearrange("p e h -> p (e h)")
                    pe.matmul(S[a][:, :], w1_a, xh_t[:, c, :], start=True, stop=True).then_inc(hid_projected, 1)

            def transpose_mask(c):
                pe.wait_ge(onehot_ready, c + 1)
                pe.wait_ge(xh_t_ready, CHUNKS if c == 3 else 3)
                if c == 2:
                    pe.wait_ge(x2_ready, B)
                need(pe, mask_t_ready, c)
                for s in range(4):
                    ins = pe.matmul(TB[0:PARTS * E, s * P:(s + 1) * P],
                                    onehot[:, c, s, :, :].rearrange("p a e -> p (a e)"), ident_bf[:, :],
                                    start=True, stop=True)
                ins.then_inc(mask_transposed, 1)

            def expand_mask(c):
                pe.wait_ge(mask_t_ready, c + 1)
                if c == 0:
                    pe.wait_ge(exps_done, LASTG * BANKS)
                for a in range(HB):
                    need(pe, hid_masked, HB * (c - 1) + a + 1)
                    pe.matmul(S[2 + a][:, :], expand[0:E, a, :], mask_bf[0:E, c % 2, :],
                              start=True, stop=True).then_inc(masks_projected, 1)

            def down(c):
                need(pe, y_ready, c)
                pe.wait_ge(logits_copied, 3 if c < 2 else CHUNKS)
                if c == 0:
                    pe.wait_ge(b2_parts_loaded, 16 * PARTS)
                for a in range(HB):
                    pe.wait_ge(hid_masked, HB * c + a + 1)
                for s in range(4):
                    o = PB[:, s * D:(s + 1) * D]
                    for a in range(HB):
                        pe.matmul(o, hid_m[:, c % 2, a, s * P:(s + 1) * P], w2_sb[:, a, :], start=(a == 0), stop=False)
                    ins = pe.matmul(o, mask_bf[0:PARTS * E, c % 2, s * P:(s + 1) * P], b2_parts[0:PARTS * E, :],
                                    start=False, stop=True)
                ins.then_inc(y_projected, 1)

            def ffn_step(G, k):
                if (G, k) == (LASTG - 4, 5):
                    transpose_xh(0)
                if (G, k) == (LASTG - 3, 1):
                    project_logits(0)
                if (G, k) == (LASTG - 3, 3):
                    transpose_xh(1)
                if (G, k) == (LASTG - 3, 7):
                    project_logits(1)
                if (G, k) == (LASTG - 2, 7):
                    transpose_xh(2)
                if (G, k) == (LASTG - 1, 2):
                    project_logits(2)
                if (G, k) == (LASTG - 1, 7):
                    transpose_mask(0)
                if (G, k) == (LASTG, 0):
                    hidden(0)
                if (G, k) == (LASTG, 7):
                    expand_mask(0)
                if (G, k) == (LASTG + 1, 3):
                    hidden(1)
                    transpose_mask(1)
                if (G, k) == (LASTG + 2, 0):
                    down(0)
                    pe.wait_ge(mask_t_ready, 2)
                if (G, k) == (LASTG + 2, 1):
                    expand_mask(1)
                if (G, k) == (LASTG + 2, 3):
                    hidden(2)

            schedule(pe, step, ffn_weights)
            down(1)
            transpose_mask(2)
            expand_mask(2)
            transpose_xh(3)
            project_logits(3)
            hidden(3)
            transpose_mask(3)
            down(2)
            expand_mask(3)
            down(3)


_INS = ["x", "ctx_1024", "L0_xattn_Wq", "L0_xattn_Wk", "L0_xattn_Wv", "L0_xattn_Wo", "L0_ffn_Wg",
        "L0_ffn_ln_scale", "L0_ffn_ln_bias", "L0_ffn_W1", "L0_ffn_b1", "L0_ffn_W2", "L0_ffn_b2"]


def kernel(**inputs):
    import numpy as _np
    import concourse.bacc as _bacc
    from concourse import mybir as _mybir
    from concourse.bass_utils import run_bass_kernel_spmd as _run

    nc = _bacc.Bacc("TRN2", target_bir_lowering=False, num_devices=1)
    arrays, args = {}, []
    for name in _INS:
        a = _np.ascontiguousarray(inputs[name])
        arrays[f"in_{name}"] = a
        args.append(nc.dram_tensor(f"in_{name}", a.shape, _mybir.dt.from_np(a.dtype), kind="ExternalInput").ap())
    x = arrays["in_x"]
    args.append(nc.dram_tensor("out_0", x.shape, _mybir.dt.from_np(x.dtype), kind="ExternalOutput").ap())
    cross_attention_moe(nc, *args)
    r = _run(nc, [arrays], core_ids=[0])
    return r.results[0]["out_0"]
```

```python
import concourse.bass as bass
from concourse import mybir
from contextlib import ExitStack

F32 = mybir.dt.float32
BF16 = mybir.dt.bfloat16
ALU = mybir.AluOpType
ACT = mybir.ActivationFunctionType
AX = mybir.AxisListType

P = 128
HEADS = 16
LN_EPS = 1e-5
PARTS = 3
GH = 4
DVE_BANKS = 4


def cross_attention_moe(nc, x, ctx, Wq, Wk, Wv, Wo, Wg, ln_scale, ln_bias, W1, b1, W2, b2, out):
    B, N, D = x.shape
    L = ctx.shape[1]
    C = D // HEADS
    NB, LB = N // P, L // P
    GROUPS = HEADS // GH
    BANKS = GH * LB // 2
    KROWS = PARTS * PARTS * C
    TERM = PARTS * C
    E, H = b1.shape
    EH = E * H
    HB = EH // P
    T = B * NB
    TILES = (2 * NB,) * (B // 2 - 1) + (NB, NB)
    FIRST = tuple(sum(TILES[:c]) for c in range(len(TILES)))
    CHUNKS = len(TILES)
    WIDE = 2 * NB
    WARMUPS = 6
    SMALL = 4
    SCALE = float(D) ** -0.5
    RING = DVE_BANKS
    LASTG = B * GROUPS
    HALF = HEADS // 2
    LOADS = 2

    k_parts_dram = nc.dram_tensor("k_parts_dram", [PARTS, P, L], BF16, kind="Internal").ap()
    q_parts_dram = nc.dram_tensor("q_parts_dram", [PARTS, PARTS, P, N], BF16, kind="Internal").ap()

    with ExitStack() as stack:
        def sb(name, shape, dt=F32):
            return stack.enter_context(nc.sbuf_tensor(name, shape, dt))

        def bank(name):
            return stack.enter_context(nc.psum_tensor(name, [P, 512], F32))

        def sem(name):
            return stack.enter_context(nc.semaphore(name))

        ident = sb("ident", [P, P])
        ident_bf = sb("ident_bf", [P, P], BF16)
        w_in = sb("w_in", [P, 4, D])
        w_t = sb("w_t", [P, 4, D])
        x_all = sb("x_all", [P, B, NB, D])
        x2_all = sb("x2_all", [P, B, NB, D])
        ctx_in = sb("ctx_in", [P, LB, D])
        ctx_t = sb("ctx_t", [P, L])
        stats = sb("stats", [P, NB, 6])
        mean_var = sb("mean_var", [P, NB, 2])
        rstd = sb("rstd", [P, NB])
        minus_half = sb("minus_half", [P, T])
        eps = sb("eps", [P, NB])
        zero = sb("zero", [P, 1])
        xm = sb("xm", [P, NB, D])
        warm = sb("warm", [P, 1])
        busy = sb("busy", [P, 512], BF16)
        xn = sb("xn", [P, NB, D])
        xn_t = sb("xn_t", [P, N])
        kf = sb("kf", [P, L])
        qf = sb("qf", [P, N])
        k_rest = sb("k_rest", [P, L])
        q_rest = sb("q_rest", [P, N])
        k_parts = sb("k_parts", [P, PARTS, L], BF16)
        q_parts = sb("q_parts", [P, PARTS, N], BF16)
        k_stack = sb("k_stack", [P, HEADS, L], BF16)
        q_stack = sb("q_stack", [P, HEADS, N], BF16)
        v_ones = sb("v_ones", [P, LB, HEADS, C + 1])
        v_hat = sb("v_hat", [P, GROUPS, GH, LB, 32])
        neg_max = sb("neg_max", [P, BANKS, 2])
        row_sum = sb("row_sum", [P, GROUPS, GH * LB])
        recip_sum = sb("recip_sum", [P, GROUPS, GH * LB])
        expd = sb("expd", [P, GROUPS, GH, LB, N])
        o_sb = sb("o_sb", [P, N])
        recip_den = sb("recip_den", [P, NB, GH])
        o_n = sb("o_n", [P, NB, D])
        o_t = sb("o_t", [P, N])

        wg_t = sb("wg_t", [P, E])
        scale_t = sb("scale_t", [P, E])
        bias_t = sb("bias_t", [P, E])
        w1_raw = sb("w1_raw", [P, E, H])
        w1_s = sb("w1_s", [P, E, H])
        b1_col = sb("b1_col", [P, HB])
        w2_sb = sb("w2_sb", [P, HB, D])
        b2_sb = sb("b2_sb", [E, D])
        b2_rest = sb("b2_rest", [E, D])
        b2_split = sb("b2_split", [E, PARTS, D], BF16)
        b2_parts = sb("b2_parts", [PARTS * E, D], BF16)
        own = sb("own", [P, HB, E])
        own_bias = sb("own_bias", [P, HB, E])
        bias_sum = sb("bias_sum", [P, HB])
        hid_bias = sb("hid_bias", [P, HB])
        xh = sb("xh", [P, B, NB, D])
        xh_t = sb("xh_t", [P, CHUNKS, WIDE * P])
        logits = sb("logits", [P, 4, E])
        top = sb("top", [P, 4])
        first = sb("first", [P, 4, E])
        ftop = sb("ftop", [P, 4])
        order = sb("order", [P, E])
        onehot = sb("onehot", [P, CHUNKS, 4, PARTS, E], BF16)
        hid = sb("hid", [P, 2, HB, 512])
        hid_m = sb("hid_m", [P, 2, HB, 512])
        mask_bf = sb("mask_bf", [PARTS * E, 2, 512], BF16)
        expand = sb("expand", [E, HB, P], BF16)
        stats2 = sb("stats2", [P, NB, 6])
        mean_var2 = sb("mean_var2", [P, NB, 2])
        f_tmp = sb("f_tmp", [P, SMALL, NB])
        x2m = sb("x2m", [P, NB, D])
        y_sb = sb("y_sb", [P, 2, 4, D])

        S = [bank(f"scores{i}") for i in range(RING)]
        O = bank("o_acc")
        TB = bank("transposes")
        PB = bank("projections")
        M = bank("mixed")

        (busy_filled, consts_ready, ident_ready, filled, v_filled, ffn_consts, stats2_done, moments2_ready,
         wq_loaded, wk_loaded, w_vo_loaded, x0_loaded, x_rest_loaded, ctx_loaded, small_loaded, w_transposed,
         w_ready, stats_done, moments_ready, eps_added, rstd_ready, mean_taken, xn_ready, xn_transposed, xn_t_ready,
         ctx_transposed, ctx_t_ready, k_projected, k_copied, q_projected, q_copied, v_projected, v_copied,
         k_split, q_split, k_parts_ready, q_parts_ready, k_stored, q_stored, first_loaded, half0_loaded, half1_loaded,
         scores_ready, max_ready, exps_done, recip_ready, v_hat_ready, pv_done, o_copied, o_transposed,
         den_ready, o_normed, o_t_transposed, o_t_copied, wo_projected, x2_ready) = [
            sem(n) for n in (
                "busy_filled consts_ready ident_ready filled v_filled ffn_consts stats2_done moments2_ready "
                "wq_loaded wk_loaded w_vo_loaded x0_loaded x_rest_loaded ctx_loaded small_loaded w_transposed "
                "w_ready stats_done moments_ready eps_added rstd_ready mean_taken xn_ready xn_transposed xn_t_ready "
                "ctx_transposed ctx_t_ready k_projected k_copied q_projected q_copied v_projected v_copied "
                "k_split q_split k_parts_ready q_parts_ready k_stored q_stored first_loaded half0_loaded half1_loaded "
                "scores_ready max_ready exps_done recip_ready v_hat_ready pv_done o_copied o_transposed "
                "den_ready o_normed o_t_transposed o_t_copied wo_projected x2_ready").split()]
        (f_small, x2_centred, xh_ready, xh_transposed, xh_t_ready, hid_projected, gelu_done,
         logits_projected, logits_copied, top_done, first_done, ftop_done, onehot_ready, mask_transposed, masks_projected, mask_t_ready,
         hid_masked, y_projected, y_ready, y_stored0, y_stored1, w1_scaled, bias_projected, bias_masked, bias_summed,
         hid_bias_ready, b2_stage, b2_split_ready, b2_parts_loaded) = [
            sem(n) for n in (
                "f_small x2_centred xh_ready xh_transposed xh_t_ready hid_projected gelu_done "
                "logits_projected logits_copied top_done first_done ftop_done onehot_ready mask_transposed masks_projected mask_t_ready "
                "hid_masked y_projected y_ready y_stored0 y_stored1 w1_scaled bias_projected bias_masked bias_summed "
                "hid_bias_ready b2_stage b2_split_ready b2_parts_loaded").split()]

        half_loaded = (half0_loaded, half1_loaded)
        y_stored = (y_stored0, y_stored1)

        def need(eng, semaphore, value):
            if not isinstance(value, int) or value > 0:
                eng.wait_ge(semaphore, value)

        AHEAD = 3
        V_AT = (0, 2, 4, 5)
        PV_AT = ((1, 5), (1, 7), (2, 1), (2, 3))
        LOOPS = B - 2

        def schedule(eng, step, before=None):
            for G in range(AHEAD):
                if G == 2 and before is not None:
                    before()
                step(G, 0, G)
            with eng.Fori(0, LOOPS) as r:
                for i in range(AHEAD, AHEAD + GROUPS):
                    step(r * GROUPS + i, r + i // GROUPS, i % GROUPS)
            for G in range(LOOPS * GROUPS + AHEAD, LASTG + AHEAD):
                step(G, G // GROUPS, G % GROUPS)

        def stages_next(G):
            return not isinstance(G, int) or G // GROUPS + 1 < B

        def norms_ahead(G):
            return not isinstance(G, int) or G // GROUPS + 2 < B

        def finishes(G):
            return not isinstance(G, int) or G >= GROUPS

        def live(G):
            return not isinstance(G, int) or 0 <= G < LASTG

        def split(eng, full, rest, parts, stage_done, ready, b, first_made=False):
            zeros = zero[0:full.shape[0], :].to_broadcast([full.shape[0], full.shape[1]])
            if not first_made:
                eng.tensor_tensor(parts[:, 0, :], full[:, :], zeros, ALU.add).then_inc(stage_done, 1)
            eng.wait_ge(stage_done, 3 * b + 1)
            eng.tensor_tensor(rest[:, :], full[:, :], parts[:, 0, :], ALU.subtract).then_inc(stage_done, 1)
            eng.wait_ge(stage_done, 3 * b + 2)
            eng.tensor_tensor(parts[:, 1, :], rest[:, :], zeros, ALU.add).then_inc(stage_done, 1)
            eng.wait_ge(stage_done, 3 * b + 3)
            eng.tensor_tensor(parts[:, 2, :], rest[:, :], parts[:, 1, :], ALU.subtract).then_inc(ready, 1)

        block = stack.enter_context(nc.Block())

        @block.sync
        def _(sp):
            def load_ctx(b):
                sp.dma_start(ctx_in[:, :, :], ctx[b].rearrange("(k p) d -> p k d", p=P)).then_inc(ctx_loaded, 16)

            def heads_of(half):
                return slice(half * HALF, (half + 1) * HALF)

            def load_k(half, heads=None, loaded=None):
                heads, loaded = heads or heads_of(half), loaded or half_loaded[half]
                kd = k_parts_dram.rearrange("b (c h) l -> (b c) h l", h=HEADS)[:, heads, :]
                kd = kd.unsqueeze(0).to_broadcast([PARTS, TERM, heads.stop - heads.start, L])
                sp.dma_start(k_stack[0:KROWS, heads, :], kd).then_inc(loaded, 16)

            def load_q(half, heads=None, loaded=None):
                heads, loaded = heads or heads_of(half), loaded or half_loaded[half]
                qd = q_parts_dram.rearrange("a b (c h) n -> (a b c) h n", h=HEADS)[:, heads, :]
                sp.dma_start(q_stack[0:KROWS, heads, :], qd).then_inc(loaded, 16)

            def store_k(b, wait=True):
                sp.wait_ge(k_parts_ready, b + 1)
                sp.dma_start(k_parts_dram.rearrange("b p l -> p b l"), k_parts[:, :, :]).then_inc(k_stored, 16)
                if wait:
                    sp.wait_ge(k_stored, (b + 1) * 16)

            def store_q_copy(b, t):
                sp.wait_ge(q_parts_ready, b + 1)
                sp.dma_start(q_parts_dram[:, t].rearrange("a p n -> p a n"), q_parts[:, :, :]).then_inc(q_stored, 16)

            def store_q(b):
                for t in range(PARTS):
                    store_q_copy(b, t)
                sp.wait_ge(q_stored, (b + 1) * 16 * PARTS)

            sp.dma_start(w_in[:, 1, :], Wk).then_inc(wk_loaded, 16)
            load_ctx(0)
            sp.dma_start(x_all[:, 0, :, :], x[0].rearrange("(s p) d -> p s d", p=P)).then_inc(x0_loaded, 16)
            sp.dma_start(w_in[:, 0, :], Wq).then_inc(wq_loaded, 16)
            for i, w in enumerate((Wv, Wo)):
                sp.dma_start(w_in[:, 2 + i, :], w).then_inc(w_vo_loaded, 16)
            for b in range(1, B):
                sp.dma_start(x_all[:, b, :, :], x[b].rearrange("(s p) d -> p s d", p=P)).then_inc(x_rest_loaded, 16)
            sp.wait_ge(ctx_transposed, 1)
            load_ctx(1)
            store_k(0, wait=False)
            for t in range(PARTS):
                store_q_copy(0, t)
            sp.wait_ge(k_stored, 16)
            load_k(0, slice(0, GH), first_loaded)
            sp.wait_ge(q_stored, 16 * PARTS)
            load_q(0, slice(0, GH), first_loaded)
            load_k(0, slice(GH, HALF))
            load_q(0, slice(GH, HALF))
            load_k(1)
            load_q(1)
            with nc.allow_non_contiguous_dma(reason="small weights"):
                sp.dma_start(wg_t[:, :], Wg.rearrange("e d -> d e")).then_inc(small_loaded, 16)
                sp.dma_start(scale_t[:, :], ln_scale.rearrange("e d -> d e")).then_inc(small_loaded, 16)
                sp.dma_start(bias_t[:, :], ln_bias.rearrange("e d -> d e")).then_inc(small_loaded, 16)
                sp.dma_start(w1_raw[:, :, :], W1.rearrange("e d h -> d e h")).then_inc(small_loaded, 16)
                sp.dma_start(b1_col[:, :], b1.rearrange("(a e) h -> (e h) a", a=HB)).then_inc(small_loaded, 16)
            sp.dma_start(w2_sb[:, :, :], W2.rearrange("(a e) h d -> (e h) a d", a=HB)).then_inc(small_loaded, 16)
            sp.dma_start(b2_sb[:, :], b2).then_inc(small_loaded, 16)

            def batch(b, more):
                if more:
                    sp.wait_ge(ctx_transposed, b + 2)
                    load_ctx(b + 2)
                sp.wait_ge(half0_loaded, (b + 1) * 16 * LOADS)
                sp.wait_ge(half1_loaded, (b + 1) * 16 * LOADS)
                store_k(b + 1)
                sp.wait_ge(scores_ready, (b * GROUPS + 2) * BANKS)
                load_k(0)
                store_q(b + 1)
                load_q(0)
                sp.wait_ge(scores_ready, (b * GROUPS + 4) * BANKS)
                load_k(1)
                load_q(1)

            sp.wait_ge(first_loaded, 16 * LOADS)
            with sp.Fori(0, B - 2) as b:
                batch(b, True)
            batch(B - 2, False)
            sp.wait_ge(b2_split_ready, 1)
            for a in range(PARTS):
                sp.dma_start(b2_parts[a * E:(a + 1) * E, :], b2_split[:, a, :]).then_inc(b2_parts_loaded, 16)
            for c in range(CHUNKS):
                sp.wait_ge(y_ready, c + 1)
                first, n = FIRST[c], TILES[c]
                sp.dma_start(out[first // NB:(first + n) // NB].rearrange("b (s p) d -> p (b s) d", p=P),
                             y_sb[:, c % 2, 0:n, :]).then_inc(y_stored[c % 2], 16)
            sp.wait_ge(y_stored0, 16 * ((CHUNKS + 1) // 2))
            sp.wait_ge(y_stored1, 16 * (CHUNKS // 2))

        @block.gpsimd
        def _(pool):
            for m in (ident, ident_bf):
                pool.memset(m[:, :], 0.0).then_inc(filled, 1)
            pool.wait_ge(filled, 2)
            for m in (ident, ident_bf):
                pool.affine_select(out=m[:, :], in_=m[:, :], compare_op=ALU.not_equal, fill=1.0, base=0,
                                   pattern=[[-1, P]], channel_multiplier=1).then_inc(ident_ready, 1)
            pool.memset(minus_half[:, :], -0.5).then_inc(consts_ready, 1)
            pool.memset(eps[:, :], LN_EPS).then_inc(consts_ready, 1)
            pool.memset(zero[:, :], 0.0).then_inc(consts_ready, 1)
            pool.wait_ge(consts_ready, 3)

            def make_rstd(b):
                pool.wait_ge(moments_ready, 2 * (b + 1))
                need(pool, xn_ready, b)
                pool.tensor_tensor(rstd[:, :], mean_var[:, :, 1], eps[:, :], ALU.add).then_inc(eps_added, 1)
                pool.wait_ge(eps_added, b + 1)
                pool.tensor_tensor(rstd[:, :], rstd[:, :], minus_half[:, 0:NB], ALU.pow).then_inc(rstd_ready, 1)

            def split_k(b):
                pool.wait_ge(k_copied, b + 1)
                need(pool, k_stored, 16 * b)
                split(pool, kf, k_rest, k_parts, k_split, k_parts_ready, b)

            def split_q(b):
                pool.wait_ge(q_copied, b + 1)
                need(pool, q_stored, 16 * PARTS * b)
                split(pool, qf, q_rest, q_parts, q_split, q_parts_ready, b,
                      first_made=isinstance(b, int) and b == 0)

            def make_v_hat(G, b, g):
                pool.wait_ge(recip_ready, G + 1)
                pool.wait_ge(v_copied, b + 1)
                slot = g
                pool.tensor_tensor(
                    v_hat[:, slot, :, :, 0:C + 1],
                    v_ones[:, :, GH * g:GH * g + GH, :].rearrange("p l h c -> p h l c"),
                    recip_sum[:, slot, :].rearrange("p (h l) -> p h l", h=GH).unsqueeze(3)
                    .to_broadcast([P, GH, LB, C + 1]),
                    ALU.mult).then_inc(v_hat_ready, 1)

            def x_norm(b):
                pool.tensor_tensor(xm[:, :, :], x_all[:, b, :, :],
                                   mean_var[:, :, 0:1].to_broadcast([P, NB, D]), ALU.subtract).then_inc(mean_taken, 1)
                pool.wait_ge(mean_taken, b - 1)
                pool.tensor_tensor(xn[:, :, :], xm[:, :, :], rstd[:, :].unsqueeze(2).to_broadcast([P, NB, D]),
                                   ALU.mult).then_inc(xn_ready, 1)

            make_rstd(0)
            pool.memset(v_ones[:, :, :, :], 1.0).then_inc(v_filled, 1)
            split_q(0)
            make_rstd(1)
            pool.memset(v_hat[:, :, :, :, :], 0.0).then_inc(v_filled, 1)
            for e in range(E):
                pool.memset(order[:, e:e + 1], float(E - e)).then_inc(ffn_consts, 1)
            pool.memset(own[:, :, :], 1.0).then_inc(filled, 1)
            pool.memset(expand[:, :, :], 1.0).then_inc(filled, 1)
            pool.wait_ge(filled, 4)
            pool.affine_select(out=own[:, :, :], in_=own[:, :, :], compare_op=ALU.is_ge, fill=0.0, base=0,
                               pattern=[[P, HB], [-H, E]], channel_multiplier=1).then_inc(filled, 1)
            pool.affine_select(out=expand[:, :, :], in_=expand[:, :, :], compare_op=ALU.is_ge, fill=0.0, base=0,
                               pattern=[[P, HB], [1, P]], channel_multiplier=-H).then_inc(filled, 1)
            pool.wait_ge(filled, 6)
            pool.affine_select(out=own[:, :, :], in_=own[:, :, :], compare_op=ALU.is_ge, fill=0.0, base=H - 1,
                               pattern=[[-P, HB], [H, E]], channel_multiplier=-1).then_inc(ffn_consts, 1)
            pool.affine_select(out=expand[:, :, :], in_=expand[:, :, :], compare_op=ALU.is_ge, fill=0.0, base=H - 1,
                               pattern=[[-P, HB], [-1, P]], channel_multiplier=H).then_inc(ffn_consts, 1)
            pool.wait_ge(v_filled, 2)

            def ffn_norm(b):
                mean, var = mean_var2[:, :, 0:1], mean_var2[:, :, 1]
                pool.wait_ge(moments2_ready, 2 * (b + 1))
                half = minus_half[:, 0:NB]
                done = b * SMALL

                def chained(out, in0, in1, op):
                    nonlocal done
                    done = done + 1
                    pool.tensor_tensor(out, in0, in1, op).then_inc(f_small, 1)
                    pool.wait_ge(f_small, done)

                chained(f_tmp[:, 0, :], var, eps[:, :], ALU.add)
                chained(f_tmp[:, 1, :], f_tmp[:, 0, :], eps[:, :], ALU.mult)
                chained(f_tmp[:, 2, :], f_tmp[:, 1, :], var, ALU.add)
                chained(f_tmp[:, 3, :], f_tmp[:, 2, :], half, ALU.pow)
                if isinstance(b, int) and b == B - 1:
                    return
                pool.tensor_tensor(x2m[:, :, :], x2_all[:, b, :, :], mean.to_broadcast([P, NB, D]),
                                   ALU.subtract).then_inc(x2_centred, 1)
                pool.wait_ge(x2_centred, b + 1)
                pool.tensor_tensor(xh[:, b, :, :], x2m[:, :, :],
                                   f_tmp[:, 3, :].unsqueeze(2).to_broadcast([P, NB, D]), ALU.mult).then_inc(xh_ready, 1)

            def step(G, b, g):
                if live(G - 1):
                    make_v_hat(G - 1, b - 1 if g == 0 else b, (g - 1) % GROUPS)
                if g == 1 and stages_next(G):
                    split_k(b + 1)
                if g == 2:
                    if stages_next(G):
                        split_q(b + 1)
                    if finishes(G):
                        ffn_norm(b - 1)
                if g == 3 and norms_ahead(G):
                    pool.wait_ge(xn_transposed, b + 2)
                    make_rstd(b + 2)
                    x_norm(b + 2)

            def split_b2():
                pool.wait_ge(small_loaded, 7 * 16)
                split(pool, b2_sb, b2_rest, b2_split, b2_stage, b2_split_ready, 0)

            schedule(pool, step, split_b2)

        @block.vector
        def _(dve):
            def x_stats(b):
                if isinstance(b, int) and b == 0:
                    dve.wait_ge(x0_loaded, 16)
                else:
                    dve.wait_ge(x_rest_loaded, 16 * (B - 1))
                    dve.wait_ge(xn_ready, b)
                for s in range(NB):
                    dve.bn_stats(stats[:, s, :], x_all[:, b, s, :]).then_inc(stats_done, 1)

            def x_moments():
                for s in range(NB):
                    dve.bn_aggr(mean_var[:, s, :], stats[:, s, :]).then_inc(moments_ready, 1)

            def x_norm(b):
                dve.wait_ge(moments_ready, 2 * (b + 1))
                dve.wait_ge(rstd_ready, b + 1)
                need(dve, xn_transposed, b)
                for s in range(NB):
                    ins = dve.tensor_scalar(xn[:, s, :], x_all[:, b, s, :], mean_var[:, s, 0:1], rstd[:, s:s + 1],
                                            ALU.subtract, ALU.mult)
                ins.then_inc(xn_ready, 1)

            def copy_ctx_t(b):
                dve.wait_ge(ctx_transposed, b + 1)
                need(dve, v_projected, b)
                dve.tensor_copy(ctx_t[:, :], TB[:, :]).then_inc(ctx_t_ready, 1)

            def copy_k(b):
                dve.wait_ge(k_projected, b + 1)
                need(dve, k_parts_ready, b)
                dve.tensor_copy(kf[:, :], PB[:, :]).then_inc(k_copied, 1)

            def copy_xn_t(b):
                dve.wait_ge(xn_transposed, b + 1)
                need(dve, q_projected, b)
                dve.tensor_copy(xn_t[:, :], TB[:, 0:N]).then_inc(xn_t_ready, 1)

            def copy_q(b):
                dve.wait_ge(q_projected, b + 1)
                need(dve, q_parts_ready, b)
                dve.tensor_scalar(qf[:, :], PB[:, 0:N], SCALE, None, ALU.mult).then_inc(q_copied, 1)

            def copy_v(b):
                dve.wait_ge(v_projected, b + 1)
                need(dve, v_hat_ready, b * GROUPS)
                dve.tensor_copy(v_ones[:, :, :, 0:C],
                                PB[:, :].rearrange("p (l h c) -> p l h c", l=LB, h=HEADS)).then_inc(v_copied, 1)

            dve.memset(busy[:, :], 0.0).then_inc(busy_filled, 1)
            x_stats(0)
            dve.wait_ge(stats_done, NB)
            x_moments()
            x_norm(0)
            dve.wait_ge(xn_transposed, 1)
            dve.tensor_copy(xn_t[:, :], S[0][:, 0:N]).then_inc(xn_t_ready, 1)
            dve.wait_ge(consts_ready, 3)
            dve.wait_ge(k_copied, 1)
            split(dve, kf, k_rest, k_parts, k_split, k_parts_ready, 0, first_made=True)
            x_stats(1)
            dve.wait_ge(stats_done, 2 * NB)
            x_moments()
            x_norm(1)

            def step(G, b, g):
                for k in range(BANKS):
                    if live(G):
                        if g == 3 and k == 3 and norms_ahead(G):
                            dve.wait_ge(stats_done, (b + 3) * NB)
                        if g == 2 and k == 6 and finishes(G):
                            dve.wait_ge(x2_ready, b)
                            need(dve, xh_ready, b - 1)
                        if g == 2 and k == 7 and finishes(G):
                            dve.wait_ge(stats2_done, b * NB)
                        dve.wait_ge(scores_ready, G * BANKS + k + 1)
                        dve.tensor_reduce(neg_max[:, k, :], S[k % RING][:, :].rearrange("p (j n) -> p j n", j=2),
                                          AX.X, ALU.max, negate=True).then_inc(max_ready, 1)
                    if k == 3 and live(G - 2):
                        dve.wait_ge(pv_done, G - 1)
                        need(dve, o_transposed, G - 2)
                        dve.tensor_copy(o_sb[:, :], O[:, 0:N]).then_inc(o_copied, 1)
                    if k == 7 and live(G - 2):
                        g2 = (g - 2) % GROUPS
                        dve.wait_ge(o_transposed, G - 1)
                        o_view = M[:, 0:NB * P].rearrange("p (s h c) -> p s h c", s=NB, h=GH)
                        dve.reciprocal(recip_den[:, :, :], o_view[:, :, :, C]).then_inc(den_ready, 1)
                        dve.wait_ge(den_ready, G - 1)
                        if g2 == 0:
                            need(dve, o_t_transposed, b)
                        dve.tensor_tensor(
                            o_n[:, :, g2 * GH * C:(g2 + 1) * GH * C].rearrange("p s (h c) -> p s h c", h=GH),
                            o_view[:, :, :, 0:C],
                            recip_den[:, :, :].unsqueeze(3).to_broadcast([P, NB, GH, C]),
                            ALU.mult).then_inc(o_normed, 1)
                    if k == 1 and live(G - 1):
                        slot = (g - 1) % GROUPS
                        dve.wait_ge(exps_done, G * BANKS)
                        dve.reciprocal(recip_sum[:, slot, :], row_sum[:, slot, :]).then_inc(recip_ready, 1)
                    if g == 0 and live(G):
                        if k == 6:
                            copy_v(b)
                        if stages_next(G) and k == 4:
                            copy_ctx_t(b + 1)
                    if g == 3 and live(G) and norms_ahead(G):
                        if k == 1:
                            x_stats(b + 2)
                        if k == 4:
                            x_moments()
                    if g == 1 and stages_next(G):
                        if k == 4:
                            copy_xn_t(b + 1)
                        if k == 4:
                            copy_k(b + 1)
                    if g == 2 and k == 0 and stages_next(G):
                        copy_q(b + 1)
                    if g == 2 and finishes(G):
                            if k == 1:
                                dve.wait_ge(o_t_transposed, b)
                                dve.tensor_copy(o_t[:, :], TB[:, 0:N]).then_inc(o_t_copied, 1)
                            if k == 4:
                                dve.wait_ge(wo_projected, b)
                                dve.tensor_tensor(x2_all[:, b - 1, :, :], x_all[:, b - 1, :, :],
                                                  TB[:, 0:N].rearrange("p (s d) -> p s d", s=NB),
                                                  ALU.add).then_inc(x2_ready, 1)
                            if k == 6:
                                if not live(G):
                                    dve.wait_ge(x2_ready, b)
                                for s in range(NB):
                                    dve.bn_stats(stats2[:, s, :], x2_all[:, b - 1, s, :]).then_inc(stats2_done, 1)
                            if k == 7:
                                if not live(G):
                                    dve.wait_ge(stats2_done, b * NB)
                                for s in range(NB):
                                    dve.bn_aggr(mean_var2[:, s, :], stats2[:, s, :]).then_inc(moments2_ready, 1)
                    if isinstance(G, int):
                        ffn_step(G, k)

            def ffn_weights():
                dve.wait_ge(small_loaded, 7 * 16)
                dve.wait_ge(ffn_consts, E + 2)
                dve.tensor_tensor(w1_s[:, :, :], w1_raw[:, :, :], scale_t[:, :].unsqueeze(2).to_broadcast([P, E, H]),
                                  ALU.mult).then_inc(w1_scaled, 1)
                dve.wait_ge(bias_projected, 1)
                dve.tensor_tensor(own_bias[:, :, :], own[:, :, :],
                                  M[:, 0:HB * E].rearrange("p (a e) -> p a e", a=HB), ALU.mult).then_inc(bias_masked, 1)
                dve.wait_ge(bias_masked, 1)
                dve.tensor_reduce(bias_sum[:, :], own_bias[:, :, :], AX.X, ALU.add).then_inc(bias_summed, 1)
                dve.wait_ge(bias_summed, 1)
                dve.tensor_tensor(hid_bias[:, :], bias_sum[:, :], b1_col[:, :], ALU.add).then_inc(hid_bias_ready, 1)

            x2_tiles = x2_all[:, :, :, :].rearrange("p b s d -> p (b s) d")

            def copy_xh_t(c):
                dve.wait_ge(xh_transposed, c + 1)
                n = TILES[c] * P
                dve.tensor_copy(xh_t[:, c, 0:n], TB[:, 0:n]).then_inc(xh_t_ready, 1)

            def normalise_last():
                dve.wait_ge(f_small, SMALL * B)
                for s in range(NB):
                    ins = dve.tensor_scalar(xh[:, B - 1, s, :], x2_all[:, B - 1, s, :], mean_var2[:, s, 0:1],
                                            f_tmp[:, SMALL - 1, s:s + 1], ALU.subtract, ALU.mult)
                ins.then_inc(xh_ready, 1)

            def route(c):
                n = TILES[c]
                bank_ = TB if c == CHUNKS - 1 else PB
                dve.wait_ge(logits_projected, c + 1)
                dve.tensor_copy(logits[:, 0:n, :],
                                bank_[:, 0:n * E].rearrange("p (s e) -> p s e", s=n)).then_inc(logits_copied, 1)
                dve.wait_ge(logits_copied, c + 1)
                dve.tensor_reduce(top[:, 0:n], logits[:, 0:n, :], AX.X, ALU.max).then_inc(top_done, 1)
                dve.wait_ge(top_done, c + 1)
                dve.tensor_tensor(first[:, 0:n, :], logits[:, 0:n, :], top[:, 0:n].unsqueeze(2).to_broadcast([P, n, E]),
                                  ALU.is_equal).then_inc(first_done, 1)
                dve.wait_ge(first_done, 2 * c + 1)
                dve.tensor_tensor(first[:, 0:n, :], first[:, 0:n, :], order[:, :].unsqueeze(1).to_broadcast([P, n, E]),
                                  ALU.mult).then_inc(first_done, 1)
                dve.wait_ge(first_done, 2 * c + 2)
                dve.tensor_reduce(ftop[:, 0:n], first[:, 0:n, :], AX.X, ALU.max).then_inc(ftop_done, 1)
                dve.wait_ge(ftop_done, c + 1)
                dve.tensor_tensor(onehot[:, c, 0:n, :, :],
                                  first[:, 0:n, :].unsqueeze(2).to_broadcast([P, n, PARTS, E]),
                                  ftop[:, 0:n].unsqueeze(2).unsqueeze(3).to_broadcast([P, n, PARTS, E]),
                                  ALU.is_equal).then_inc(onehot_ready, 1)

            def mask_hidden(c):
                n = TILES[c] * P
                for a in range(HB):
                    dve.wait_ge(masks_projected, HB * c + a + 1)
                    dve.wait_ge(gelu_done, HB * c + a + 1)
                    need(dve, y_projected, c - 1)
                    dve.tensor_tensor(hid_m[:, c % 2, a, 0:n], hid[:, c % 2, a, 0:n], S[2 + a][:, 0:n],
                                      ALU.mult).then_inc(hid_masked, 1)

            def finish(c):
                n = TILES[c]
                dve.wait_ge(y_projected, c + 1)
                need(dve, y_stored[c % 2], 16 * (c // 2))
                dve.tensor_tensor(y_sb[:, c % 2, 0:n, :], x2_tiles[:, FIRST[c]:FIRST[c] + n, :],
                                  PB[:, 0:n * D].rearrange("p (s d) -> p s d", s=n), ALU.add).then_inc(y_ready, 1)

            def ffn_step(G, k):
                if (G, k) == (LASTG - 4, 7):
                    copy_xh_t(0)
                if (G, k) == (LASTG - 3, 3):
                    route(0)
                if (G, k) == (LASTG - 3, 5):
                    copy_xh_t(1)
                if (G, k) == (LASTG - 2, 1):
                    route(1)
                if (G, k) == (LASTG - 1, 0):
                    copy_xh_t(2)
                if (G, k) == (LASTG - 1, 4):
                    route(2)
                if (G, k) == (LASTG, 0):
                    copy_xh_t(3)
                if (G, k) == (LASTG, 6):
                    route(3)
                if (G, k) == (LASTG + 1, 6):
                    mask_hidden(0)
                if (G, k) == (LASTG + 2, 3):
                    finish(0)

            schedule(dve, step, ffn_weights)
            mask_hidden(1)
            normalise_last()
            finish(1)
            copy_xh_t(4)
            mask_hidden(2)
            route(4)
            finish(2)
            mask_hidden(3)
            finish(3)
            mask_hidden(4)
            finish(4)

        @block.scalar
        def _(act):
            def step(G, b, g):
                if not live(G):
                    return
                slot = g
                for k in range(BANKS):
                    act.wait_ge(max_ready, G * BANKS + k + 1)
                    for j in range(2):
                        hq, lb = k // 2, 2 * (k % 2) + j
                        i = hq * LB + lb
                        ins = act.activation(expd[:, slot, hq, lb, :], S[k % RING][:, j * N:(j + 1) * N], ACT.Exp,
                                             bias=neg_max[:, k, j:j + 1], scale=1.0,
                                             accum_out=row_sum[:, slot, i:i + 1])
                    ins.then_inc(exps_done, 1)

            def copy_weight(i, bank_, place, transposed):
                act.wait_ge(w_transposed, transposed)
                src = bank_[:, place * D:(place + 1) * D]
                dst = w_t[:, i, :]
                if i < 2:
                    src = src.rearrange("p (h c) -> p h c", h=HEADS)
                    dst = dst.rearrange("p (c h) -> p h c", h=HEADS)
                act.activation(dst, src, ACT.Copy).then_inc(w_ready, 1)

            act.wait_ge(consts_ready, 3)
            act.activation(warm[:, :], zero[:, :], ACT.Exp)
            copy_weight(1, M, 0, 1)
            act.wait_ge(ctx_transposed, 1)
            act.activation(ctx_t[:, :], TB[:, :], ACT.Copy).then_inc(ctx_t_ready, 1)
            copy_weight(0, S[3], 0, 2)
            act.wait_ge(k_projected, 1)
            act.activation(k_parts[:, 0, :], PB[:, :], ACT.Copy).then_inc(k_split, 1)
            act.activation(kf[:, :], PB[:, :], ACT.Copy).then_inc(k_copied, 1)
            act.wait_ge(q_projected, 1)
            act.activation(qf[:, :], S[1][:, 0:N], ACT.Copy, scale=SCALE).then_inc(q_copied, 1)
            act.activation(q_parts[:, 0, :], S[1][:, 0:N], ACT.Copy, scale=SCALE).then_inc(q_split, 1)
            copy_weight(2, S[2], 0, 4)
            copy_weight(3, S[2], 1, 4)

            schedule(act, step)

            def copy_mask(c):
                n = TILES[c] * P
                act.wait_ge(mask_transposed, c + 1)
                need(act, y_projected, c - 1)
                act.activation(mask_bf[:, c % 2, 0:n], (TB if c == 0 else O)[0:PARTS * E, 0:n],
                               ACT.Copy).then_inc(mask_t_ready, 1)

            def gelu(c):
                n = TILES[c] * P
                need(act, hid_masked, HB * (c - 1))
                for a in range(HB):
                    act.wait_ge(hid_projected, HB * c + a + 1)
                    act.activation(hid[:, c % 2, a, 0:n], S[a][:, 0:n], ACT.Gelu, bias=hid_bias[:, a:a + 1],
                                   scale=1.0).then_inc(gelu_done, 1)

            act.wait_ge(hid_bias_ready, 1)
            copy_mask(0)
            gelu(0)
            for c in range(1, CHUNKS):
                gelu(c)
                copy_mask(c)

        @block.tensor
        def _(pe):
            def transpose(o, i):
                return pe.transpose(o, i, ident[:, :])

            def transpose_weight(i, bank_, place):
                transpose(bank_[:, place * D:(place + 1) * D], w_in[:, i, :]).then_inc(w_transposed, 1)

            def transpose_ctx(b):
                pe.wait_ge(ctx_loaded, 16 * (b + 1))
                need(pe, xn_t_ready, b)
                for k in range(LB):
                    ins = transpose(TB[:, k * P:(k + 1) * P], ctx_in[:, k, :])
                ins.then_inc(ctx_transposed, 1)

            def project_k(b, half):
                pe.wait_ge(ctx_t_ready, b + 1)
                need(pe, v_copied, b)
                cols = slice(half * L // 2, (half + 1) * L // 2)
                ins = pe.matmul(PB[:, cols], w_t[:, 1, :], ctx_t[:, cols], start=True, stop=True)
                if half == 1:
                    ins.then_inc(k_projected, 1)

            def transpose_xn(b):
                first = isinstance(b, int) and b == 0
                pe.wait_ge(xn_ready, b + 1)
                if not first:
                    pe.wait_ge(ctx_t_ready, b + 1)
                for s in range(NB):
                    ins = transpose((S[0] if first else TB)[:, s * P:(s + 1) * P], xn[:, s, :])
                ins.then_inc(xn_transposed, 1)

            def project_q(b):
                first = isinstance(b, int) and b == 0
                pe.wait_ge(xn_t_ready, b + 1)
                if not first:
                    pe.wait_ge(k_copied, b + 1)
                pe.matmul((S[1] if first else PB)[:, 0:N], w_t[:, 0, :], xn_t[:, :],
                          start=True, stop=True).then_inc(q_projected, 1)

            def project_v(b, k):
                pe.wait_ge(q_copied, b + 1)
                if isinstance(b, int) and b == 0:
                    pe.wait_ge(k_copied, 1)
                ins = pe.matmul(PB[:, k * P:(k + 1) * P], ctx_t[:, k * P:(k + 1) * P], w_t[:, 2, :],
                                start=True, stop=True)
                if k == LB - 1:
                    ins.then_inc(v_projected, 1)

            pe.wait_ge(busy_filled, 1)
            for i in range(WARMUPS):
                pe.matmul(S[0][:, :], busy[:, 0:P], busy[:, :], start=True, stop=True)
            pe.wait_ge(ident_ready, 2)
            pe.wait_ge(wk_loaded, 16)
            transpose_weight(1, M, 0)
            transpose_ctx(0)
            pe.wait_ge(wq_loaded, 16)
            transpose_weight(0, S[3], 0)
            pe.wait_ge(w_ready, 1)
            project_k(0, 0)
            transpose_xn(0)
            project_k(0, 1)
            pe.wait_ge(w_ready, 2)
            project_q(0)
            pe.wait_ge(w_vo_loaded, 32)
            transpose_weight(2, S[2], 0)
            transpose_weight(3, S[2], 1)
            pe.wait_ge(w_ready, 4)

            def step(G, b, g):
                for k in range(BANKS):
                    if live(G):
                        if k == 0 and isinstance(G, int) and G < 2:
                            pe.wait_ge((first_loaded, half0_loaded)[G], 16 * LOADS)
                        elif k == 0 and g == 0:
                            pe.wait_ge(half0_loaded, (b + 1) * 16 * LOADS)
                        if k == 0 and g == GROUPS // 2:
                            pe.wait_ge(half1_loaded, (b + 1) * 16 * LOADS)
                        need(pe, exps_done, G * BANKS + k + 1 - RING)
                        h = GH * g + k // 2
                        for j in range(2):
                            lb = 2 * (k % 2) + j
                            ins = pe.matmul(S[k % RING][:, j * N:(j + 1) * N],
                                            k_stack[0:KROWS, h, lb * P:(lb + 1) * P],
                                            q_stack[0:KROWS, h, :], start=True, stop=True)
                        ins.then_inc(scores_ready, 1)
                    if k == 6 and live(G - 2):
                        pe.wait_ge(o_copied, G - 1)
                        need(pe, o_normed, G - 2)
                        for s in range(NB):
                            ins = transpose(M[:, s * P:(s + 1) * P], o_sb[:, s * P:(s + 1) * P])
                        ins.then_inc(o_transposed, 1)
                    if g == 0 and live(G):
                        if k in V_AT:
                            project_v(b, V_AT.index(k))
                        if k == 3 and stages_next(G):
                            transpose_ctx(b + 1)
                    if g == 1 and stages_next(G):
                        if k == 2:
                            project_k(b + 1, 0)
                        if k == 2:
                            transpose_xn(b + 1)
                        if k == 4:
                            project_k(b + 1, 1)
                        if k == 7:
                            project_q(b + 1)
                    if g == 2 and finishes(G):
                        if k == 1:
                            pe.wait_ge(o_normed, G - 2)
                            for s in range(NB):
                                ins = transpose(TB[:, s * P:(s + 1) * P], o_n[:, s, :])
                            ins.then_inc(o_t_transposed, 1)
                        if k == 4:
                            pe.wait_ge(o_t_copied, b)
                            for s in range(NB):
                                ins = pe.matmul(TB[:, s * P:(s + 1) * P], o_t[:, s * P:(s + 1) * P], w_t[:, 3, :],
                                                start=True, stop=True)
                            ins.then_inc(wo_projected, 1)
                    for lb, (lag, at) in enumerate(PV_AT):
                        if at != k or not live(G - lag):
                            continue
                        slot = (g - lag) % GROUPS
                        if lb == 0:
                            pe.wait_ge(v_hat_ready, G)
                            need(pe, o_copied, G - 1)
                        for hq in range(GH):
                            ins = pe.matmul(O[32 * hq:32 * hq + 32, 0:N], v_hat[:, slot, hq, lb, :],
                                            expd[:, slot, hq, lb, :], start=(lb == 0), stop=(lb == LB - 1),
                                            tile_position=(0, 32 * hq))
                        if lb == LB - 1:
                            ins.then_inc(pv_done, 1)
                    if isinstance(G, int):
                        ffn_step(G, k)

            def ffn_weights():
                pe.wait_ge(small_loaded, 7 * 16)
                for a in range(HB):
                    ins = pe.matmul(M[:, a * E:(a + 1) * E],
                                    w1_raw[:, a * (E // HB):(a + 1) * (E // HB), :].rearrange("p e h -> p (e h)"),
                                    bias_t[:, :], start=True, stop=True)
                ins.then_inc(bias_projected, 1)
                pe.wait_ge(bias_masked, 1)

            def transpose_xh(c):
                first, n = FIRST[c], TILES[c]
                pe.wait_ge(xh_ready, (first + n) // NB)
                need(pe, xh_t_ready, c)
                if c == 2:
                    pe.wait_ge(x2_ready, B - 1)
                if c == CHUNKS - 1:
                    pe.wait_ge(mask_t_ready, 1)
                for s in range(n):
                    ins = transpose(TB[:, s * P:(s + 1) * P], xh[:, (first + s) // NB, (first + s) % NB, :])
                ins.then_inc(xh_transposed, 1)

            def project_logits(c):
                bank_ = TB if c == CHUNKS - 1 else PB
                pe.wait_ge(xh_t_ready, c + 1)
                need(pe, logits_copied, c)
                if c == 0:
                    pe.wait_ge(v_copied, B)
                for s in range(TILES[c]):
                    ins = pe.matmul(bank_[:, s * E:(s + 1) * E], xh_t[:, c, s * P:(s + 1) * P], wg_t[:, :],
                                    start=True, stop=True)
                ins.then_inc(logits_projected, 1)

            def hidden(c):
                n = TILES[c] * P
                pe.wait_ge(xh_t_ready, c + 1)
                if c == 0:
                    pe.wait_ge(w1_scaled, 1)
                for a in range(HB):
                    if c == 0:
                        pe.wait_ge(exps_done, LASTG * BANKS - RING + a + 1)
                    need(pe, gelu_done, HB * (c - 1) + a + 1)
                    w1_a = w1_s[:, a * (E // HB):(a + 1) * (E // HB), :].rearrange("p e h -> p (e h)")
                    pe.matmul(S[a][:, 0:n], w1_a, xh_t[:, c, 0:n], start=True, stop=True).then_inc(hid_projected, 1)

            def transpose_mask(c):
                pe.wait_ge(onehot_ready, c + 1)
                if c == 0:
                    pe.wait_ge(xh_t_ready, 4)
                else:
                    pe.wait_ge(o_copied, LASTG)
                    pe.wait_ge(mask_t_ready, c)
                for s in range(TILES[c]):
                    ins = pe.matmul((TB if c == 0 else O)[0:PARTS * E, s * P:(s + 1) * P],
                                    onehot[:, c, s, :, :].rearrange("p a e -> p (a e)"), ident_bf[:, :],
                                    start=True, stop=True)
                ins.then_inc(mask_transposed, 1)

            def expand_mask(c):
                n = TILES[c] * P
                pe.wait_ge(mask_t_ready, c + 1)
                if c == 0:
                    pe.wait_ge(exps_done, LASTG * BANKS)
                for a in range(HB):
                    need(pe, hid_masked, HB * (c - 1) + a + 1)
                    pe.matmul(S[2 + a][:, 0:n], expand[0:E, a, :], mask_bf[0:E, c % 2, 0:n],
                              start=True, stop=True).then_inc(masks_projected, 1)

            def down(c):
                need(pe, y_ready, c)
                pe.wait_ge(logits_copied, CHUNKS - 1)
                if c == 0:
                    pe.wait_ge(b2_parts_loaded, 16 * PARTS)
                for a in range(HB):
                    pe.wait_ge(hid_masked, HB * c + a + 1)
                for s in range(TILES[c]):
                    o = PB[:, s * D:(s + 1) * D]
                    for a in range(HB):
                        pe.matmul(o, hid_m[:, c % 2, a, s * P:(s + 1) * P], w2_sb[:, a, :], start=(a == 0), stop=False)
                    ins = pe.matmul(o, mask_bf[0:PARTS * E, c % 2, s * P:(s + 1) * P], b2_parts[0:PARTS * E, :],
                                    start=False, stop=True)
                ins.then_inc(y_projected, 1)

            def ffn_step(G, k):
                if (G, k) == (LASTG - 4, 5):
                    transpose_xh(0)
                if (G, k) == (LASTG - 3, 1):
                    project_logits(0)
                if (G, k) == (LASTG - 3, 3):
                    transpose_xh(1)
                if (G, k) == (LASTG - 3, 7):
                    project_logits(1)
                if (G, k) == (LASTG - 2, 7):
                    transpose_xh(2)
                if (G, k) == (LASTG - 1, 2):
                    project_logits(2)
                if (G, k) == (LASTG - 1, 7):
                    transpose_xh(3)
                if (G, k) == (LASTG, 0):
                    hidden(0)
                    transpose_mask(0)
                if (G, k) == (LASTG, 5):
                    project_logits(3)
                if (G, k) == (LASTG, 7):
                    expand_mask(0)
                if (G, k) == (LASTG + 1, 3):
                    hidden(1)
                if (G, k) == (LASTG + 1, 7):
                    transpose_mask(1)
                if (G, k) == (LASTG + 2, 0):
                    pe.wait_ge(mask_t_ready, 1)
                if (G, k) == (LASTG + 2, 2):
                    down(0)
                if (G, k) == (LASTG + 2, 5):
                    expand_mask(1)
                    hidden(2)
                    transpose_mask(2)
                    down(1)

            schedule(pe, step, ffn_weights)
            transpose_xh(4)
            expand_mask(2)
            hidden(3)
            transpose_mask(3)
            project_logits(4)
            down(2)
            hidden(4)
            expand_mask(3)
            transpose_mask(4)
            down(3)
            expand_mask(4)
            down(4)


_INS = ["x", "ctx_1024", "L0_xattn_Wq", "L0_xattn_Wk", "L0_xattn_Wv", "L0_xattn_Wo", "L0_ffn_Wg",
        "L0_ffn_ln_scale", "L0_ffn_ln_bias", "L0_ffn_W1", "L0_ffn_b1", "L0_ffn_W2", "L0_ffn_b2"]


def kernel(**inputs):
    import numpy as _np
    import concourse.bacc as _bacc
    from concourse import mybir as _mybir
    from concourse.bass_utils import run_bass_kernel_spmd as _run

    nc = _bacc.Bacc("TRN2", target_bir_lowering=False, num_devices=1)
    arrays, args = {}, []
    for name in _INS:
        a = _np.ascontiguousarray(inputs[name])
        arrays[f"in_{name}"] = a
        args.append(nc.dram_tensor(f"in_{name}", a.shape, _mybir.dt.from_np(a.dtype), kind="ExternalInput").ap())
    x = arrays["in_x"]
    args.append(nc.dram_tensor("out_0", x.shape, _mybir.dt.from_np(x.dtype), kind="ExternalOutput").ap())
    cross_attention_moe(nc, *args)
    r = _run(nc, [arrays], core_ids=[0])
    return r.results[0]["out_0"]
```
